# Optimizing a Trainium2 kernel written in Bass

```python
import numpy as np
import jax
import jax.numpy as jnp

def _softmax(x, axis=-1):
    return jax.nn.softmax(x, axis=axis)

def _gelu(x):
    return jax.nn.gelu(x, approximate=True)

def _silu(x):
    return jax.nn.silu(x)

def _sigmoid(x):
    return jax.nn.sigmoid(x)

def _layernorm(x, axis=-1, eps=1e-05):
    m = jnp.mean(x, axis=axis, keepdims=True)
    v = jnp.var(x, axis=axis, keepdims=True)
    return (x - m) / jnp.sqrt(v + eps)

def _scatter_add(tgt, idx, src, axis=0):
    return tgt.at[idx].add(src)

def _segment_sum(src, seg, n):
    return jax.ops.segment_sum(src, seg, n)
kernel_name = 'mk_pixart_resid_d2_seqx_r8_5c3262'

def setup_inputs(seed: int=0):
    np.random.seed(seed)
    _w = jnp.asarray

    def _rec_inputs():
        import jax
        import jax.numpy as jnp
        _rk = jax.random.key(seed)
        x = -0.0002928 + 1 * jax.random.normal(jax.random.fold_in(_rk, 1), (2, 512, 128), jnp.float32)
        _lenS = 512 - jax.random.randint(jax.random.fold_in(_rk, 7), (2,), 0, max(1, 512 // 4) + 1, jnp.int32)
        _lenS2 = 154 - jax.random.randint(jax.random.fold_in(_rk, 8), (2,), 0, max(1, 154 // 4) + 1, jnp.int32)
        _ctx_1024P = jax.random.normal(jax.random.fold_in(_rk, 11), (2, 16, 128), jnp.float32)
        _ctx_1024c = jax.random.dirichlet(jax.random.fold_in(_rk, 511), 0.3 * jnp.ones((16,), jnp.float32), (2, 154))
        _ctx_1024t = jnp.einsum('bsk,bkd->bsd', _ctx_1024c, _ctx_1024P)
        _ctx_1024t = _ctx_1024t * jax.lax.rsqrt(jnp.mean(jnp.square(_ctx_1024t)) + 1e-12) * 0.953939
        ctx_1024 = -1.52775e-05 + 0.999936 * (_ctx_1024t + 0.3 * jax.random.normal(jax.random.fold_in(_rk, 611), (2, 154, 128), jnp.float32))
        cond_1024 = -0.00779384 + 0.997222 * jax.random.normal(jax.random.fold_in(_rk, 12), (2, 128), jnp.float32)
        return (x, ctx_1024, cond_1024)
    x, ctx_1024, cond_1024 = _rec_inputs()

    def _L0_xcond_setup():
        import jax, jax.numpy as jnp
        import numpy as np
        B, T, S, H, E = (128, 32, 32, 128, 128)
        key = jax.random.key(seed)
        ks = jax.random.split(key, 8)
        sc = lambda n: 1.0 / np.sqrt(n)
        return dict(dec_seq=jax.random.normal(ks[0], (B, T, E), jnp.float32), enc_hiddens=jax.random.normal(ks[1], (B, S, H), jnp.float32), last_hidden=jax.random.normal(ks[2], (B, H), jnp.float32), W_att=jax.random.normal(ks[3], (2 * H, H), jnp.float32) * sc(2 * H), V_att=jax.random.normal(ks[4], (H, 1), jnp.float32) * sc(H), Wi=jax.random.normal(ks[5], (E + H, 3 * H), jnp.float32) * sc(E + H), Uh=jax.random.normal(ks[6], (H, 3 * H), jnp.float32) * sc(H), b=jnp.zeros((3 * H,), jnp.float32))
    _L0_xcond_all = _L0_xcond_setup()
    _L0_xcond_in = {k: v for k, v in _L0_xcond_all.items() if k in ('W_att', 'V_att', 'Wi', 'Uh', 'b')}
    del _L0_xcond_all

    def _L0_ffn_setup():
        import jax, jax.numpy as jnp
        import numpy as np
        B, N, D = (4, 512, 128)
        E, S, F = (16, 64, 256)
        DO = 128
        EPS = 1e-05

        def _layernorm(x, g, b):
            mu = jnp.mean(x, axis=-1, keepdims=True)
            var = jnp.mean(jnp.square(x - mu), axis=-1, keepdims=True)
            return (x - mu) * jax.lax.rsqrt(var + EPS) * g + b
        key = jax.random.key(seed)
        ks = jax.random.split(key, 8)
        d = {'x': jax.random.normal(ks[0], (B, N, D), dtype=jnp.float32), 'norm_g': jnp.ones((D,), jnp.float32), 'norm_b': jnp.zeros((D,), jnp.float32), 'slot_g': jnp.ones((D,), jnp.float32), 'slot_b': jnp.zeros((D,), jnp.float32), 'scale': jnp.ones((1,), jnp.float32), 'slot_embeds': jax.random.normal(ks[1], (E, S, D), jnp.float32) / np.sqrt(D), 'Wg': jax.random.normal(ks[2], (E, D, F), jnp.float32) * np.sqrt(2.0 / (D + F)), 'bg': jnp.zeros((E, F), jnp.float32), 'Wu': jax.random.normal(ks[3], (E, D, F), jnp.float32) * np.sqrt(2.0 / (D + F)), 'bu': jnp.zeros((E, F), jnp.float32), 'Wd': jax.random.normal(ks[4], (E, F, DO), jnp.float32) * np.sqrt(2.0 / (F + DO)), 'bd': jnp.zeros((E, DO), jnp.float32)}
        return d
    _L0_ffn_all = _L0_ffn_setup()
    _L0_ffn_in = {k: v for k, v in _L0_ffn_all.items() if k in ('norm_g', 'norm_b', 'slot_g', 'slot_b', 'scale', 'slot_embeds', 'Wg', 'bg', 'Wu', 'bu', 'Wd', 'bd')}
    del _L0_ffn_all

    def _L1_xcond_setup():
        import jax, jax.numpy as jnp
        import numpy as np
        B, N, K, D, T = (16, 512, 16, 128, 3)
        EPS_ATTN = 1e-08
        LN_EPS = 1e-05

        def _ln(x, g, b):
            mu = jnp.mean(x, axis=-1, keepdims=True)
            var = jnp.mean(jnp.square(x - mu), axis=-1, keepdims=True)
            return (x - mu) * jax.lax.rsqrt(var + LN_EPS) * g + b
        key = jax.random.key(seed)
        ks = jax.random.split(key, 16)
        w = lambda k, i, o: jax.random.normal(k, (i, o), jnp.float32) * 0.02
        inp = {'x_cls': jax.random.normal(ks[0], (B, D), jnp.float32), 'x': jax.random.normal(ks[1], (B, N, D), jnp.float32), 'noise': jax.random.normal(ks[2], (B, K, D), jnp.float32), 'q_mu': jax.random.normal(ks[3], (1, 1, D), jnp.float32), 'q_logsig': jax.random.normal(ks[4], (1, 1, D), jnp.float32) * 0.02, 'lnkv_g': jnp.ones((D,), jnp.float32), 'lnkv_b': jnp.zeros((D,), jnp.float32), 'lnq_g': jnp.ones((D,), jnp.float32), 'lnq_b': jnp.zeros((D,), jnp.float32), 'lnm_g': jnp.ones((D,), jnp.float32), 'lnm_b': jnp.zeros((D,), jnp.float32), 'lnp_g': jnp.ones((D,), jnp.float32), 'lnp_b': jnp.zeros((D,), jnp.float32), 'wk': w(ks[5], D, D), 'bk': jnp.zeros((D,), jnp.float32), 'wv': w(ks[6], D, D), 'bv': jnp.zeros((D,), jnp.float32), 'wq': w(ks[7], D, D), 'bq': jnp.zeros((D,), jnp.float32), 'wu': w(ks[8], D, D), 'bu': jnp.zeros((D,), jnp.float32), 'w1': w(ks[9], D, D), 'b1': jnp.zeros((D,), jnp.float32), 'w2': w(ks[10], D, D), 'b2': jnp.zeros((D,), jnp.float32)}
        return inp
    _L1_xcond_all = _L1_xcond_setup()
    _L1_xcond_in = {k: v for k, v in _L1_xcond_all.items() if k in ('q_mu', 'q_logsig', 'lnkv_g', 'lnkv_b', 'lnq_g', 'lnq_b', 'lnm_g', 'lnm_b', 'lnp_g', 'lnp_b', 'wk', 'bk', 'wv', 'bv', 'wq', 'bq', 'wu', 'bu', 'w1', 'b1', 'w2', 'b2')}
    del _L1_xcond_all

    def _L1_ffn_setup():
        import jax, jax.numpy as jnp
        import numpy as np
        TOP_K = 2
        E = 8
        D = 128
        F = 256
        B, S = (2, 128)
        key = jax.random.key(seed)
        ks = jax.random.split(key, 8)
        sc = 0.02
        return {'x_bsD': jax.random.normal(ks[0], (B, S, D), dtype=jnp.float32), 'router_DE': jax.random.normal(ks[1], (D, E), dtype=jnp.float32) * sc, 'w_in_shared_FD': jax.random.normal(ks[2], (F, D), dtype=jnp.float32) * sc, 'w_out_shared_DF': jax.random.normal(ks[3], (D, F), dtype=jnp.float32) * sc, 'w_swiglu_FD': jax.random.normal(ks[4], (F, D), dtype=jnp.float32) * sc, 'w_in_eDF': jax.random.normal(ks[5], (E, D, F), dtype=jnp.float32) * sc, 'w_swiglu_eDF': jax.random.normal(ks[6], (E, D, F), dtype=jnp.float32) * sc, 'w_out_eFD': jax.random.normal(ks[7], (E, F, D), dtype=jnp.float32) * sc}
    _L1_ffn_all = _L1_ffn_setup()
    _L1_ffn_in = {k: v for k, v in _L1_ffn_all.items() if k in ('router_DE', 'w_in_shared_FD', 'w_out_shared_DF', 'w_swiglu_FD', 'w_in_eDF', 'w_swiglu_eDF', 'w_out_eFD')}
    del _L1_ffn_all
    return {'x': x, 'ctx_1024': ctx_1024, 'cond_1024': cond_1024, 'L0_xcond_W_att': _L0_xcond_in['W_att'], 'L0_xcond_V_att': _L0_xcond_in['V_att'], 'L0_xcond_Wi': _L0_xcond_in['Wi'], 'L0_xcond_Uh': _L0_xcond_in['Uh'], 'L0_xcond_b': _L0_xcond_in['b'], 'L0_ffn_norm_g': _L0_ffn_in['norm_g'], 'L0_ffn_norm_b': _L0_ffn_in['norm_b'], 'L0_ffn_slot_g': _L0_ffn_in['slot_g'], 'L0_ffn_slot_b': _L0_ffn_in['slot_b'], 'L0_ffn_scale': _L0_ffn_in['scale'], 'L0_ffn_slot_embeds': _L0_ffn_in['slot_embeds'], 'L0_ffn_Wg': _L0_ffn_in['Wg'], 'L0_ffn_bg': _L0_ffn_in['bg'], 'L0_ffn_Wu': _L0_ffn_in['Wu'], 'L0_ffn_bu': _L0_ffn_in['bu'], 'L0_ffn_Wd': _L0_ffn_in['Wd'], 'L0_ffn_bd': _L0_ffn_in['bd'], 'L1_xcond_q_mu': _L1_xcond_in['q_mu'], 'L1_xcond_q_logsig': _L1_xcond_in['q_logsig'], 'L1_xcond_lnkv_g': _L1_xcond_in['lnkv_g'], 'L1_xcond_lnkv_b': _L1_xcond_in['lnkv_b'], 'L1_xcond_lnq_g': _L1_xcond_in['lnq_g'], 'L1_xcond_lnq_b': _L1_xcond_in['lnq_b'], 'L1_xcond_lnm_g': _L1_xcond_in['lnm_g'], 'L1_xcond_lnm_b': _L1_xcond_in['lnm_b'], 'L1_xcond_lnp_g': _L1_xcond_in['lnp_g'], 'L1_xcond_lnp_b': _L1_xcond_in['lnp_b'], 'L1_xcond_wk': _L1_xcond_in['wk'], 'L1_xcond_bk': _L1_xcond_in['bk'], 'L1_xcond_wv': _L1_xcond_in['wv'], 'L1_xcond_bv': _L1_xcond_in['bv'], 'L1_xcond_wq': _L1_xcond_in['wq'], 'L1_xcond_bq': _L1_xcond_in['bq'], 'L1_xcond_wu': _L1_xcond_in['wu'], 'L1_xcond_bu': _L1_xcond_in['bu'], 'L1_xcond_w1': _L1_xcond_in['w1'], 'L1_xcond_b1': _L1_xcond_in['b1'], 'L1_xcond_w2': _L1_xcond_in['w2'], 'L1_xcond_b2': _L1_xcond_in['b2'], 'L1_ffn_router_DE': _L1_ffn_in['router_DE'], 'L1_ffn_w_in_shared_FD': _L1_ffn_in['w_in_shared_FD'], 'L1_ffn_w_out_shared_DF': _L1_ffn_in['w_out_shared_DF'], 'L1_ffn_w_swiglu_FD': _L1_ffn_in['w_swiglu_FD'], 'L1_ffn_w_in_eDF': _L1_ffn_in['w_in_eDF'], 'L1_ffn_w_swiglu_eDF': _L1_ffn_in['w_swiglu_eDF'], 'L1_ffn_w_out_eFD': _L1_ffn_in['w_out_eFD']}

def reference(x, ctx_1024, cond_1024, L0_xcond_W_att, L0_xcond_V_att, L0_xcond_Wi, L0_xcond_Uh, L0_xcond_b, L0_ffn_norm_g, L0_ffn_norm_b, L0_ffn_slot_g, L0_ffn_slot_b, L0_ffn_scale, L0_ffn_slot_embeds, L0_ffn_Wg, L0_ffn_bg, L0_ffn_Wu, L0_ffn_bu, L0_ffn_Wd, L0_ffn_bd, L1_xcond_q_mu, L1_xcond_q_logsig, L1_xcond_lnkv_g, L1_xcond_lnkv_b, L1_xcond_lnq_g, L1_xcond_lnq_b, L1_xcond_lnm_g, L1_xcond_lnm_b, L1_xcond_lnp_g, L1_xcond_lnp_b, L1_xcond_wk, L1_xcond_bk, L1_xcond_wv, L1_xcond_bv, L1_xcond_wq, L1_xcond_bq, L1_xcond_wu, L1_xcond_bu, L1_xcond_w1, L1_xcond_b1, L1_xcond_w2, L1_xcond_b2, L1_ffn_router_DE, L1_ffn_w_in_shared_FD, L1_ffn_w_out_shared_DF, L1_ffn_w_swiglu_FD, L1_ffn_w_in_eDF, L1_ffn_w_swiglu_eDF, L1_ffn_w_out_eFD):
    import jax
    import jax.numpy as jnp

    def _L0_xcond_ref(dec_seq, enc_hiddens, last_hidden, W_att, V_att, Wi, Uh, b):
        import jax, jax.numpy as jnp
        import numpy as np
        B, T, S, H, E = (128, 32, 32, 128, 128)
        Bn, Sn, Hn = enc_hiddens.shape

        def step(h, x_t):
            hid = jnp.broadcast_to(h[:, None, :], (Bn, Sn, Hn))
            combined = jnp.concatenate([hid, enc_hiddens], axis=2)
            score = jnp.tanh(jnp.einsum('bsk,kh->bsh', combined, W_att))
            score = jnp.einsum('bsh,h->bs', score, V_att[:, 0])
            attn = jax.nn.softmax(score, axis=-1)
            context = jnp.einsum('bs,bsh->bh', attn, enc_hiddens)
            inp = jnp.concatenate([x_t, context], axis=1)
            gz, gr, gh = jnp.split(inp @ Wi + b, 3, axis=1)
            rz, rr, rh = jnp.split(h @ Uh, 3, axis=1)
            z = jax.nn.sigmoid(gz + rz)
            r = jax.nn.sigmoid(gr + rr)
            hh = jnp.tanh(gh + r * rh)
            h_new = z * h + (1.0 - z) * hh
            return (h_new, h_new)
        _, outs = jax.lax.scan(step, last_hidden, jnp.swapaxes(dec_seq, 0, 1))
        return jnp.swapaxes(outs, 0, 1)

    def _L0_ffn_ref(x, norm_g, norm_b, slot_g, slot_b, scale, slot_embeds, Wg, bg, Wu, bu, Wd, bd):
        import jax, jax.numpy as jnp
        import numpy as np
        B, N, D = (4, 512, 128)
        E, S, F = (16, 64, 256)
        DO = 128
        EPS = 1e-05

        def _layernorm(x, g, b):
            mu = jnp.mean(x, axis=-1, keepdims=True)
            var = jnp.mean(jnp.square(x - mu), axis=-1, keepdims=True)
            return (x - mu) * jax.lax.rsqrt(var + EPS) * g + b
        x = _layernorm(x, norm_g, norm_b)
        se = _layernorm(slot_embeds, slot_g, slot_b) * scale
        logits = jnp.einsum('bnd,esd->bnes', x, se)
        dispatch = jax.nn.softmax(logits, axis=1)
        combine = jax.nn.softmax(logits.reshape(x.shape[0], x.shape[1], -1), axis=-1)
        slots = jnp.einsum('bnd,bnes->besd', x, dispatch)
        gate = jax.nn.gelu(jnp.einsum('besd,edf->besf', slots, Wg) + bg[None, :, None, :], approximate=False)
        up = jnp.einsum('besd,edf->besf', slots, Wu) + bu[None, :, None, :]
        eout = jnp.einsum('besf,efo->beso', gate * up, Wd) + bd[None, :, None, :]
        eout = eout.reshape(eout.shape[0], -1, eout.shape[-1])
        return jnp.einsum('bns,bso->bno', combine, eout)

    def _L1_xcond_ref(x_cls, x, noise, q_mu, q_logsig, lnkv_g, lnkv_b, lnq_g, lnq_b, lnm_g, lnm_b, lnp_g, lnp_b, wk, bk, wv, bv, wq, bq, wu, bu, w1, b1, w2, b2):
        import jax, jax.numpy as jnp
        import numpy as np
        B, N, K, D, T = (16, 512, 16, 128, 3)
        EPS_ATTN = 1e-08
        LN_EPS = 1e-05

        def _ln(x, g, b):
            mu = jnp.mean(x, axis=-1, keepdims=True)
            var = jnp.mean(jnp.square(x - mu), axis=-1, keepdims=True)
            return (x - mu) * jax.lax.rsqrt(var + LN_EPS) * g + b
        scale = D ** (-0.5)
        x_in = _ln(x, lnkv_g, lnkv_b)
        k = x_in @ wk + bk
        v = x_in @ wv + bv
        slots = q_mu + jnp.exp(q_logsig) * noise
        for _ in range(T):
            prev = slots
            q = _ln(slots, lnq_g, lnq_b) @ wq + bq
            logits = jnp.einsum('bnd,bkd->bnk', k, q) / scale
            attn = jax.nn.softmax(logits, axis=-1) + EPS_ATTN
            attn = attn / jnp.sum(attn, axis=1, keepdims=True)
            upd = jnp.einsum('bnk,bnd->bkd', attn, v)
            slots = upd @ wu + bu + prev
            h = _ln(slots, lnm_g, lnm_b) @ w1 + b1
            slots = jax.nn.gelu(h, approximate=False) @ w2 + b2 + slots
            slots = _ln(slots + x_cls[:, None, :], lnp_g, lnp_b)
        return slots

    def _L1_ffn_ref(x_bsD, router_DE, w_in_shared_FD, w_out_shared_DF, w_swiglu_FD, w_in_eDF, w_swiglu_eDF, w_out_eFD):
        import jax, jax.numpy as jnp
        import numpy as np
        TOP_K = 2
        E = 8
        D = 128
        F = 256
        B, S = (2, 128)
        b, s, d = x_bsD.shape
        x_aD = x_bsD.reshape(-1, d)
        a = x_aD.shape[0]
        scores_aE = x_aD @ router_DE
        topv_aK, topi_aK = jax.lax.top_k(scores_aE, TOP_K)
        masked_aE = jnp.full_like(scores_aE, -jnp.inf)
        masked_aE = masked_aE.at[jnp.arange(a)[:, None], topi_aK].set(topv_aK)
        gates_Ea = jax.nn.sigmoid(masked_aE.astype(jnp.float32)).astype(x_aD.dtype).T
        routed_in_EaD = x_aD[None, :, :] * gates_Ea[:, :, None]
        routed_in_EaD = jax.lax.stop_gradient(routed_in_EaD)
        mid_EaF = jnp.einsum('ead,edf->eaf', routed_in_EaD, w_in_eDF)
        sw_EaF = jnp.einsum('ead,edf->eaf', routed_in_EaD, w_swiglu_eDF)
        h_EaF = jax.nn.silu(mid_EaF) * sw_EaF
        out_EaD = jnp.einsum('eaf,efd->ead', h_EaF, w_out_eFD)
        shared_aF = jax.nn.silu(x_aD @ w_in_shared_FD.T) * (x_aD @ w_swiglu_FD.T)
        shared_out_aD = jax.lax.stop_gradient(shared_aF @ w_out_shared_DF.T)
        out_aD = shared_out_aD + jnp.sum(out_EaD, axis=0)
        return out_aD.reshape(b, s, d)
    x = x + _L0_xcond_ref(_layernorm(x, axis=-1), ctx_1024, cond_1024, L0_xcond_W_att, L0_xcond_V_att, L0_xcond_Wi, L0_xcond_Uh, L0_xcond_b)
    x = x + _L0_ffn_ref(_layernorm(x, axis=-1), L0_ffn_norm_g, L0_ffn_norm_b, L0_ffn_slot_g, L0_ffn_slot_b, L0_ffn_scale, L0_ffn_slot_embeds, L0_ffn_Wg, L0_ffn_bg, L0_ffn_Wu, L0_ffn_bu, L0_ffn_Wd, L0_ffn_bd)
    x = x + _L1_xcond_ref(cond_1024, ctx_1024, _layernorm(x, axis=-1), L1_xcond_q_mu, L1_xcond_q_logsig, L1_xcond_lnkv_g, L1_xcond_lnkv_b, L1_xcond_lnq_g, L1_xcond_lnq_b, L1_xcond_lnm_g, L1_xcond_lnm_b, L1_xcond_lnp_g, L1_xcond_lnp_b, L1_xcond_wk, L1_xcond_bk, L1_xcond_wv, L1_xcond_bv, L1_xcond_wq, L1_xcond_bq, L1_xcond_wu, L1_xcond_bu, L1_xcond_w1, L1_xcond_b1, L1_xcond_w2, L1_xcond_b2)
    x = x + _L1_ffn_ref(_layernorm(x, axis=-1), L1_ffn_router_DE, L1_ffn_w_in_shared_FD, L1_ffn_w_out_shared_DF, L1_ffn_w_swiglu_FD, L1_ffn_w_in_eDF, L1_ffn_w_swiglu_eDF, L1_ffn_w_out_eFD)
    return x

_drawn_inputs = setup_inputs


def setup_inputs(seed=0):
    import zlib

    import numpy as np

    out = dict(_drawn_inputs(seed))
    spreads = {'L0_xcond_b': (0.0, 0.1),
     'L0_ffn_norm_g': (1.0, 0.2),
     'L0_ffn_norm_b': (0.0, 0.1),
     'L0_ffn_slot_g': (1.0, 0.2),
     'L0_ffn_slot_b': (0.0, 0.1),
     'L0_ffn_bg': (0.0, 0.1),
     'L0_ffn_bu': (0.0, 0.1),
     'L0_ffn_bd': (0.0, 0.1),
     'L1_xcond_lnkv_g': (1.0, 0.6),
     'L1_xcond_lnkv_b': (0.0, 0.8),
     'L1_xcond_lnq_g': (1.0, 0.6),
     'L1_xcond_lnq_b': (0.0, 0.8),
     'L1_xcond_lnm_g': (1.0, 0.6),
     'L1_xcond_lnm_b': (0.0, 0.8),
     'L1_xcond_lnp_g': (1.0, 0.2),
     'L1_xcond_lnp_b': (0.0, 0.1),
     'L1_xcond_bk': (0.0, 0.8),
     'L1_xcond_bv': (0.0, 0.689),
     'L1_xcond_bq': (0.0, 0.8),
     'L1_xcond_bu': (0.0, 0.1),
     'L1_xcond_b1': (0.0, 0.8),
     'L1_xcond_b2': (0.0, 0.1)}
    factors = {'L1_xcond_q_logsig': 8.0,
     'L1_xcond_wk': 3.813,
     'L1_xcond_wq': 3.887,
     'L1_xcond_w1': 3.85,
     'L1_xcond_w2': 3.497,
     'L1_ffn_router_DE': 8.0,
     'L1_ffn_w_in_shared_FD': 8.0,
     'L1_ffn_w_out_shared_DF': 8.0,
     'L1_ffn_w_swiglu_FD': 8.0,
     'L1_ffn_w_in_eDF': 8.0,
     'L1_ffn_w_swiglu_eDF': 8.0,
     'L1_ffn_w_out_eFD': 8.0}
    for name, (base, spread) in spreads.items():
        noise = np.random.default_rng([zlib.crc32(name.encode()), seed]).standard_normal(out[name].shape)
        drawn = base * np.exp(spread * noise) if base else spread * noise
        out[name] = jnp.asarray(drawn.astype(out[name].dtype))
    for name, factor in factors.items():
        out[name] = (out[name] * factor).astype(out[name].dtype)
    return out
```

```python
from contextlib import ExitStack

import concourse.bass as bass
from concourse import mybir

F32 = mybir.dt.float32
I32 = mybir.dt.int32
BF16 = mybir.dt.bfloat16
ALU = mybir.AluOpType
ACT = mybir.ActivationFunctionType
AX = mybir.AxisListType

B, T, D = 2, 512, 128
S = 154
NT = B * T // 128
NCC = 2
CP = S // NCC
U = 8
GZ, GR, GH, RH = range(4)
EPS = 1e-5
EPS_ATTN = 1e-8
E0, SL0, F = 16, 64, 256
NS = E0 * SL0
NJ = NS // 128
ITERS = 3
QK_SCALE = float(D) ** 0.5
E1 = 8
TOP_K = 2
FC = F // 128


def build(nc, A, out):
    with ExitStack() as ctx:
        def sb(name, shape, dt=F32):
            return ctx.enter_context(nc.sbuf_tensor(name, shape, dt))

        def sem(name):
            return ctx.enter_context(nc.semaphore(name))

        psum = ctx.enter_context(nc.psum_tensor("psum", [128, 8, 512], F32))
        bank = [psum[:, i, :] for i in range(8)]

        ident = sb("ident", [128, 128])
        ones_row = sb("ones_row", [1, 128])
        zero_col = sb("zero_col", [128, 1])
        x_tok = sb("x_tok", [128, NT, D])
        ctx_tok = sb("ctx_tok", [CP, B * NCC, D])
        w_att = sb("w_att", [D, 2, D])
        v_col = sb("v_col", [D, 1])
        v_rep = sb("v_rep", [D, D])
        wi = sb("wi", [D, 2, 3 * D])
        uh = sb("uh", [D, 3 * D])
        stats = sb("stats", [128, NT, 6])
        mv = sb("mv", [128, NT, 2])
        rstd = sb("rstd", [128, NT])
        turned = sb("turned", [128, 2, B * T])
        xnT, hist = (turned[:, i, :].rearrange("p (b t) -> p b t", b=B) for i in range(2))
        eC = turned
        encT = sb("encT", [128, B, S])
        ewx = sb("ewx", [128, B, 4, S + 1])
        hring = sb("hring", [128, B, U])
        xblk = sb("xblk", [128, B, U, 4, 3])
        xg = sb("xg", [128, B, T, 3])
        b_col = sb("b_col", [D, 3])
        uh_part = sb("uh_part", [D, 3, 3 * D], BF16)
        uh_rest = sb("uh_rest", [D, 3 * D])
        h_part = sb("h_part", [128, B, 3], BF16)
        h_rest = sb("h_rest", [128, B])
        tanhT = sb("tanhT", [128, B, S])
        probs = sb("probs", [128, B, S + 1])
        junk = sb("junk", [128, B, 3, S + 1])
        nmax = sb("nmax", [128, B])
        rden = sb("rden", [128, B])
        base_h = sb("base_h", [128, B])
        tzr = sb("tzr", [128, B, 2])
        omz = sb("omz", [128, B])
        nzh = sb("nzh", [128, B])

        seT = sb("seT", [128, NS])
        cols = sb("cols", [128, 16])
        sg_col, sbias_col, scale_col = cols[:, 0:1], cols[:, 1:2], cols[:, 2:3]
        ng_col, nb_col = cols[:, 3:4], cols[:, 4:5]
        kvg_col, kvb_col, bk_col, bv_col, bq_col, b1_col = (cols[:, i:i + 1] for i in range(5, 11))
        qg_col, qb_col, mg_col, mb_col = (cols[:, i:i + 1] for i in range(11, 15))
        x1 = sb("x1", [128, NT, D])
        xB = sb("xB", [128, NT, D])
        xBT = sb("xBT", [128, B, T])
        dmax, dsum, drec = sb("dmax", [128, 16]), sb("dsum", [128, 16]), sb("drec", [128, 16])
        slotsT = sb("slotsT", [128, E0, B, SL0])
        cmax, csum, crec = sb("cmax", [128, NT]), sb("csum", [128, NT]), sb("crec", [128, NT])
        eCT = sb("eCT", [128, B, NJ, T])
        wg, wu_ = sb("wg", [128, E0, F]), sb("wu_", [128, E0, F])
        wd = sb("wd", [128, E0 * FC, D])
        bg_col, bu_col = sb("bg_col", [128, E0 * FC]), sb("bu_col", [128, E0 * FC])
        bd_rep = sb("bd_rep", [128, NJ, D])
        ga, gu = sb("ga", [128, 2, FC, 128]), sb("gu", [128, 2, FC, 128])
        eo = sb("eo", [128, NJ, B, D])
        ctxn = sb("ctxn", [CP, B * NCC, D])
        ctxnT, kT, vT = sb("ctxnT", [128, B * S]), sb("kT", [128, B * S]), sb("vT", [128, B * S])
        wk, wv, wq, wus, w1, w2 = (sb(n, [128, D]) for n in ("wk", "wv", "wq", "wus", "w1", "w2"))
        bu_rep = sb("bu_rep", [CP, D])
        vw = sb("vw", [CP, B * NCC, D + 1])
        mu_rep, sig_rep = sb("mu_rep", [128, D]), sb("sig_rep", [128, D])
        cls_rep = sb("cls_rep", [128, B, D])
        b2_rep, pg_rep, pb_rep = sb("b2_rep", [128, D]), sb("pg_rep", [128, D]), sb("pb_rep", [128, D])
        late = eCT[:].rearrange("p b j t -> p (b j t)")

        def tok_view(t, i):
            return t[:, i * NT * D:(i + 1) * NT * D].rearrange("p (t d) -> p t d", t=NT)

        def turned_view(t, i):
            return t[:, i * B * T:(i + 1) * B * T].rearrange("p (b t) -> p b t", b=B)

        lnt, x3 = tok_view(late, 0), tok_view(late, 6)
        lnT, qT, gT, yT = (turned_view(late, i) for i in (1, 2, 3, 7))
        attn = late[0:CP, 4 * B * T:6 * B * T].rearrange("p (b c t) -> p b c t", b=B, c=NCC)
        amax, asum, arec = (sb(n, [CP, B, NCC]) for n in ("amax", "asum", "arec"))
        urec = sb("urec", [128, B, 4])
        router = sb("router", [128, E1])
        sh_turned = sb("sh_turned", [128, 3, F])
        slot_tok, slot_nrm, xn_tok, shared = (tok_view(late, i) for i in range(4))
        sh_in, sh_sw = shared[:, 0:FC, :], shared[:, FC:2 * FC, :]
        sh_out = shared[:, 2 * FC:3 * FC, :].rearrange("p c d -> p (c d)")
        slotsT_flat = slotsT[:].rearrange("p e b s -> p (e b s)")
        slots, x2 = tok_view(slotsT_flat, 0), tok_view(slotsT_flat, 1)
        sc, rank, beats, gates = (sb(n, [128, NT, E1]) for n in ("sc", "rank", "beats", "gates"))
        gTr = sb("gTr", [E1, B, T])
        sel = sb("sel", [E1, E1, 128])
        wg_flat, wu_flat, wd_flat = (w[:].rearrange("p e f -> p (e f)") for w in (wg, wu_, wd))
        win = wg_flat[:, 0:E1 * F].rearrange("p (e f) -> p e f", e=E1)
        wsw = wg_flat[:, E1 * F:2 * E1 * F].rearrange("p (e f) -> p e f", e=E1)
        wout = wu_flat[:, 0:E1 * F].rearrange("p (e f) -> p e f", e=E1)
        routed, sil, hT, outT = (turned_view(wd_flat, i) for i in range(4))
        res = tok_view(wu_flat, 3)

        names = """ld_slot ld_cols ld_exp ld_c ld_rep ld_d dve_link pre_tr pre_ev sig_done sel_done
            tr_b x1_done xB_done xBT_done lt_done dmax_done dexp_done dnorm_done dtr_done dT_done ds_done slots_ev
            l_done cmax_done cexp_done ctr_done cT_act cT_dve crec_done e_mm egelu egu eo_mm eo_ev cm_mm x2_done
            yn_done tr_y yT_done r_mm gates_done_d tr_g gTr_done rep_mm routed_done m_mm silu_done h_done_d o_mm
            outT_done tr_o res_done ld_moe""".split()
        Q = {n: sem(n) for n in names}
        CQ = {n: [sem(f"c_{n}{b}") for b in range(B)] for n in
              "q_ln q_tr q_lnT q_mm q_T log_mm amax exp attn upd_mm m_ln m_tr m_lnT m_mm gelu w2_mm slots0".split()}

        rs_v, rs_a, rs_g = sb("rs_v", [128, NT]), sb("rs_a", [128, NT]), sb("rs_g", [128, NT])
        rs_w, rs_x = sb("rs_w", [128, NT]), sb("rs_x", [128, NT])
        xg_flat = xg[:].rearrange("p b t g -> p (b t g)")
        eD = xg_flat[:, 0:3 * T].rearrange("p (i t) -> p i t", i=3)
        dT = xg_flat[:, 3 * T:5 * T].rearrange("p (i t) -> p i t", i=2)

        ld_x, ld_ctx, ld_w, ld_h0 = sem("ld_x"), sem("ld_ctx"), sem("ld_w"), sem("ld_h0")
        consts_done = sem("consts_done")
        xn_done = sem("xn_done")
        halves_done = sem("halves_done")
        setup_pe, setup_ev = sem("setup_pe"), sem("setup_ev")
        out_done = sem("out_done")

        def pair(name):
            return [sem(f"{name}{b}") for b in range(B)]

        part0, rest0, part1, part2 = pair("part0"), pair("rest0"), pair("part1"), pair("part2")
        uparts_done = sem("uparts_done")
        x_part_done, xblk_ready, hist_saved = pair("x_part_done"), pair("xblk_ready"), pair("hist_saved")
        pre_done, gates_done, scores_done = pair("pre_done"), pair("gates_done"), pair("scores_done")
        tanh_done, exp_done, tzr_done, cand_done = pair("tanh_done"), pair("exp_done"), pair("tzr_done"), pair("cand_done")
        cols_done, nmax_done, rden_done, acc_zr = pair("cols_done"), pair("nmax_done"), pair("rden_done"), pair("acc_zr")
        base_done, omz_done, nzh_done, delta_done, h_done = pair("base_done"), pair("omz_done"), pair("nzh_done"), pair("delta_done"), pair("h_done")

        pre = [bank[b][:, 0:S] for b in range(B)]
        gat = [bank[2 + b][:, 0:U * 12].rearrange("p (s g i) -> p s g i", g=4, i=3) for b in range(B)]
        sco = [bank[4 + b][:, 0:S] for b in range(B)]

        acc = [bank[4 + b][:, 160:162] for b in range(B)]
        hcand = [bank[2 + b][:, 128:129] for b in range(B)]

        block = ctx.enter_context(nc.Block())

        @block.sync
        def _(sp):
            sp.dma_start(x_tok[:], A["x"].rearrange("b (t p) d -> p (b t) d", p=128)).then_inc(ld_x, 16)
            sp.dma_start(ctx_tok[:], A["ctx_1024"].rearrange("b (c p) d -> p (b c) d", p=CP)).then_inc(ld_ctx, 16)
            sp.dma_start(w_att[:], A["L0_xcond_W_att"].rearrange("(two k) m -> k two m", two=2)).then_inc(ld_w, 16)
            sp.dma_start(v_col[:], A["L0_xcond_V_att"]).then_inc(ld_w, 16)
            sp.dma_start(wi[:], A["L0_xcond_Wi"].rearrange("(two k) m -> k two m", two=2)).then_inc(ld_w, 16)
            sp.dma_start(uh[:], A["L0_xcond_Uh"]).then_inc(ld_w, 16)
            with nc.allow_non_contiguous_dma(reason="few elements"):
                sp.dma_start(b_col[:], A["L0_xcond_b"].rearrange("(g d) -> d g", d=D)).then_inc(ld_w, 16)
                sp.dma_start(hring[:, :, U - 1], A["cond_1024"].rearrange("b d -> d b")).then_inc(ld_h0, 16)
            def row(name):
                return A[name].rearrange("(a n) -> a n", a=1)

            def col(name):
                return A[name].rearrange("(n a) -> n a", a=1)

            sp.dma_start(slot_tok, A["L0_ffn_slot_embeds"].rearrange("e s d -> (e s) d").rearrange("(t p) d -> p t d", p=128)).then_inc(Q["ld_slot"], 16)
            for k, n in enumerate("L0_ffn_slot_g L0_ffn_slot_b - L0_ffn_norm_g L0_ffn_norm_b L1_xcond_lnkv_g L1_xcond_lnkv_b "
                                  "L1_xcond_bk L1_xcond_bv L1_xcond_bq L1_xcond_b1 L1_xcond_lnq_g L1_xcond_lnq_b "
                                  "L1_xcond_lnm_g L1_xcond_lnm_b".split()):
                src = row("L0_ffn_scale").to_broadcast([128, 1]) if n == "-" else col(n)
                sp.dma_start(cols[:, k:k + 1], src).then_inc(Q["ld_cols"], 16)
            for t, n in ((wk, "wk"), (wv, "wv"), (wq, "wq"), (wus, "wu"), (w1, "w1"), (w2, "w2")):
                sp.dma_start(t[:], A["L1_xcond_" + n]).then_inc(Q["ld_c"], 16)
            sp.dma_start(bu_rep[:], row("L1_xcond_bu").to_broadcast([CP, D])).then_inc(Q["ld_rep"], 16)
            sp.dma_start(mu_rep[:], A["L1_xcond_q_mu"].rearrange("a b d -> (a b) d").to_broadcast([128, D])).then_inc(Q["ld_rep"], 16)
            sp.dma_start(sig_rep[:], A["L1_xcond_q_logsig"].rearrange("a b d -> (a b) d").to_broadcast([128, D])).then_inc(Q["ld_rep"], 16)
            for b in range(B):
                sp.dma_start(cls_rep[:, b, :], A["cond_1024"][b:b + 1, :].to_broadcast([128, D])).then_inc(Q["ld_rep"], 16)
            for t, n in ((b2_rep, "b2"), (pg_rep, "lnp_g"), (pb_rep, "lnp_b")):
                sp.dma_start(t[:], row("L1_xcond_" + n).to_broadcast([128, D])).then_inc(Q["ld_rep"], 16)
            sp.dma_start(sh_in, A["L1_ffn_w_in_shared_FD"].rearrange("(c p) d -> p c d", p=128)).then_inc(Q["ld_d"], 16)
            sp.dma_start(sh_sw, A["L1_ffn_w_swiglu_FD"].rearrange("(c p) d -> p c d", p=128)).then_inc(Q["ld_d"], 16)
            sp.dma_start(sh_out, A["L1_ffn_w_out_shared_DF"]).then_inc(Q["ld_d"], 16)
            sp.dma_start(router[:], A["L1_ffn_router_DE"]).then_inc(Q["ld_d"], 16)
            sp.dma_start(wg[:], A["L0_ffn_Wg"].rearrange("e d f -> d e f")).then_inc(Q["ld_exp"], 16)
            sp.dma_start(wu_[:], A["L0_ffn_Wu"].rearrange("e d f -> d e f")).then_inc(Q["ld_exp"], 16)
            sp.dma_start(wd[:], A["L0_ffn_Wd"].rearrange("e (c p) d -> p (e c) d", p=128)).then_inc(Q["ld_exp"], 16)
            with nc.allow_non_contiguous_dma(reason="few elements"):
                sp.dma_start(bg_col[:], A["L0_ffn_bg"].rearrange("e (c p) -> p (e c)", p=128)).then_inc(Q["ld_exp"], 16)
                sp.dma_start(bu_col[:], A["L0_ffn_bu"].rearrange("e (c p) -> p (e c)", p=128)).then_inc(Q["ld_exp"], 16)
            for half in range(2):
                sp.dma_start(bd_rep[64 * half:64 * half + 64, :, :],
                             A["L0_ffn_bd"].rearrange("(j two) d -> two j d", two=2)[half:half + 1].to_broadcast([64, NJ, D])).then_inc(Q["ld_exp"], 16)
            sp.wait_ge(Q["e_mm"], E0)
            sp.dma_start(win, A["L1_ffn_w_in_eDF"].rearrange("e d f -> d e f")).then_inc(Q["ld_moe"], 16)
            sp.dma_start(wsw, A["L1_ffn_w_swiglu_eDF"].rearrange("e d f -> d e f")).then_inc(Q["ld_moe"], 16)
            sp.dma_start(wout.rearrange("p e (c d) -> p (e c) d", c=FC), A["L1_ffn_w_out_eFD"].rearrange("e (c p) d -> p (e c) d", p=128)).then_inc(Q["ld_moe"], 16)
            sp.wait_ge(Q["res_done"], 2)
            sp.dma_start(out.rearrange("b (t p) d -> p (b t) d", p=128), res).then_inc(out_done, 16)
            sp.wait_ge(out_done, 16)

        @block.gpsimd
        def _(pool):
            pool.memset(ident[:], 0.0).then_inc(consts_done, 1)
            pool.memset(ones_row[:], 1.0).then_inc(consts_done, 1)
            pool.wait_ge(consts_done, 2)
            pool.affine_select(out=ident[:], in_=ident[:], compare_op=ALU.not_equal, fill=1.0, base=0,
                               pattern=[[-1, 128]], channel_multiplier=1).then_inc(consts_done, 1)
            pool.memset(vw[:, :, D:D + 1], 1.0).then_inc(consts_done, 1)
            pool.memset(zero_col[:], 0.0).then_inc(consts_done, 1)
            pool.memset(xblk[:], 0.0).then_inc(consts_done, 1)
            pool.wait_ge(consts_done, 6)
            pool.wait_ge(setup_ev, 12)

            def next_inputs(b, t):
                pool.tensor_copy(xblk[:, b, :, 0:3, 0], xg[:, b, bass.ds(t, U), :]).then_inc(xblk_ready[b], U)

            def split_state(b, t, s):
                p = (s - 1) % U
                h = hring[:, b, p:p + 1]
                if isinstance(t, int) and t == 0:
                    pool.wait_ge(ld_h0, 16)
                else:
                    pool.wait_ge(h_done[b], t)
                    pool.wait_ge(gates_done[b], t)
                pool.tensor_tensor(h_part[:, b, 0:1], h, zero_col[:], ALU.add).then_inc(part0[b], 1)
                pool.wait_ge(part0[b], t + 1)
                pool.tensor_tensor(h_rest[:, b:b + 1], h, h_part[:, b, 0:1], ALU.subtract).then_inc(rest0[b], 1)
                pool.wait_ge(rest0[b], t + 1)
                pool.tensor_tensor(h_part[:, b, 1:2], h_rest[:, b:b + 1], zero_col[:], ALU.add).then_inc(part1[b], 1)
                pool.wait_ge(part1[b], t + 1)
                pool.tensor_tensor(h_part[:, b, 2:3], h_rest[:, b:b + 1], h_part[:, b, 1:2], ALU.subtract).then_inc(part2[b], 1)

            def save(b, t):
                pool.tensor_copy(hist[:, b, bass.ds(t, U)], hring[:, b, :]).then_inc(hist_saved[b], U)

            def block_of_steps(t0, first=False, last=False):
                for s in range(U):
                    for b in range(B):
                        split_state(b, t0 + s, s)
                        if s == 0 and not first:
                            save(b, t0 - U)
                        if s == 1 and not last:
                            next_inputs(b, t0 + U)

            for b in range(B):
                next_inputs(b, 0)
            block_of_steps(0, first=True)
            with pool.Fori(1, T // U - 1) as k:
                block_of_steps(k * U)
            block_of_steps(T - U, last=True)
            for b in range(B):
                pool.wait_ge(h_done[b], T)
                pool.tensor_copy(hist[:, b, T - U:T], hring[:, b, :]).then_inc(hist_saved[b], U)

        @block.scalar
        def _(act):
            act.wait_ge(Q["ld_rep"], 16 * 8)
            act.activation(sig_rep[:], sig_rep[:], ACT.Exp).then_inc(Q["sig_done"], 1)

            def tanh_scores(b, t):
                act.wait_ge(pre_done[b], t + 1)
                act.activation(tanhT[:, b, :], pre[b], ACT.Tanh).then_inc(tanh_done[b], 1)

            def exp_scores(b, t):
                act.wait_ge(nmax_done[b], t + 1)
                act.activation(probs[:, b, 0:S], sco[b], ACT.Exp, bias=nmax[:, b:b + 1],
                               accum_out=probs[:, b, S:S + 1]).then_inc(exp_done[b], 1)

            def gate_zr(b, t):
                act.wait_ge(acc_zr[b], t + 1)
                act.activation(tzr[:, b, :], acc[b], ACT.Tanh, scale=rden[:, b:b + 1]).then_inc(tzr_done[b], 1)

            def candidate(b, t):
                act.wait_ge(base_done[b], t + 1)
                act.wait_ge(tzr_done[b], t + 1)
                act.activation(hcand[b], tzr[:, b, 1:2], ACT.Tanh, bias=base_h[:, b:b + 1],
                               scale=ewx[:, b, RH, S:S + 1]).then_inc(cand_done[b], 1)

            def block_of_steps(t0, first=False):
                for s in range(U):
                    t = t0 + s
                    tanh_scores(0, t)
                    if not (first and s == 0):
                        gate_zr(1, t - 1)
                        candidate(1, t - 1)
                    exp_scores(0, t)
                    tanh_scores(1, t)
                    gate_zr(0, t)
                    candidate(0, t)
                    exp_scores(1, t)

            block_of_steps(0, True)
            with act.Fori(1, T // U) as k:
                block_of_steps(k * U)
            gate_zr(1, T - 1)
            candidate(1, T - 1)

            def d_exp(k):
                act.wait_ge(Q["dmax_done"], k + 1)
                if k >= 3:
                    act.wait_ge(Q["dtr_done"], k - 2)
                act.activation(eD[:, k % 3, :], bank[k % 2], ACT.Exp, bias=dmax[:, k:k + 1],
                               accum_out=dsum[:, k:k + 1]).then_inc(Q["dexp_done"], 1)

            def d_copy(k):
                act.wait_ge(Q["dtr_done"], k + 1)
                if k >= 2:
                    act.wait_ge(Q["ds_done"], k - 1)
                act.activation(dT[:, k % 2, :], bank[2 + k % 2], ACT.Copy).then_inc(Q["dT_done"], 1)

            for k in range(16 + 1):
                if k < 16:
                    d_exp(k)
                if k >= 1:
                    d_copy(k - 1)

            def c_exp(m):
                act.wait_ge(Q["cmax_done"], m + 1)
                if m >= 2:
                    act.wait_ge(Q["ctr_done"], m - 1)
                p = (6, 0)[m % 2]
                act.activation(eC[:, m % 2, :], psum[:, p:p + 2, :].rearrange("p a n -> p (a n)"), ACT.Exp, bias=cmax[:, m:m + 1],
                               accum_out=csum[:, m:m + 1]).then_inc(Q["cexp_done"], 1)

            def c_copy(m):
                act.wait_ge(Q["ctr_done"], m + 1)
                b, i = m // 4, m % 4
                act.activation(eCT[:, b, 0:4, i * 128:(i + 1) * 128], bank[2 + 2 * (m % 2)].rearrange("p (j n) -> p j n", j=4),
                               ACT.Copy).then_inc(Q["cT_act"], 1)

            for m in range(8 + 1):
                if m < 8:
                    c_exp(m)
                if m >= 1:
                    c_copy(m - 1)

            act.wait_ge(Q["ld_exp"], 16 * 7)
            for e in range(E0):
                act.wait_ge(Q["e_mm"], e + 1)
                if e >= 2:
                    act.wait_ge(Q["egu"], e - 1)
                for f in range(FC):
                    ins = act.activation(ga[:, e % 2, f, :], bank[e % 2][:, f * 128:(f + 1) * 128], ACT.Gelu,
                                         bias=bg_col[:, e * FC + f:e * FC + f + 1])
                ins.then_inc(Q["egelu"], 1)

            for it in range(ITERS):
                for b in range(B):
                    act.wait_ge(CQ["q_tr"][b], it + 1)
                    act.activation(lnT[:, b, :], bank[4 * b], ACT.Identity, bias=qb_col, scale=qg_col).then_inc(CQ["q_lnT"][b], 1)
                for b in range(B):
                    act.wait_ge(CQ["q_mm"][b], it + 1)
                    act.activation(qT[:, b, :], bank[4 * b + 1], ACT.Identity, bias=bq_col).then_inc(CQ["q_T"][b], 1)
                for b in range(B):
                    act.wait_ge(CQ["amax"][b], it + 1)
                    for c in range(NCC):
                        ins = act.activation(attn[:, b, c, :], bank[4 * b + 2 + c][0:CP, :], ACT.Exp, bias=amax[:, b, c:c + 1],
                                             scale=QK_SCALE, accum_out=asum[:, b, c:c + 1])
                    ins.then_inc(CQ["exp"][b], 1)
                for b in range(B):
                    act.wait_ge(CQ["m_tr"][b], it + 1)
                    act.activation(lnT[:, b, :], bank[4 * b + 2], ACT.Identity, bias=mb_col, scale=mg_col).then_inc(CQ["m_lnT"][b], 1)
                for b in range(B):
                    act.wait_ge(CQ["m_mm"][b], it + 1)
                    act.activation(gT[:, b, :], bank[4 * b + 3], ACT.Gelu, bias=b1_col).then_inc(CQ["gelu"][b], 1)

            for b in range(B):
                act.wait_ge(Q["tr_y"], b + 1)
                act.activation(yT[:, b, :], bank[b], ACT.Copy).then_inc(Q["yT_done"], 1)
            act.wait_ge(Q["r_mm"], 1)
            act.activation(gates[:].rearrange("p t e -> p (t e)"), bank[2][:, 0:NT * E1], ACT.Exp, scale=-1.0).then_inc(Q["gates_done_d"], 1)
            for u in range(2 * B * (E1 + 1)):
                act.wait_ge(Q["m_mm"], u + 1)
                if u >= 2:
                    act.wait_ge(Q["h_done_d"], u - 1)
                act.activation(sil[:, u % 2, :], bank[u % 2], ACT.Silu).then_inc(Q["silu_done"], 1)
            for b in range(B):
                act.wait_ge(Q["o_mm"], B * 2 * (E1 + 1) - 2 * (B - 1 - b))
                act.activation(outT[:, b, :], bank[6 + b], ACT.Copy).then_inc(Q["outT_done"], 1)

        @block.vector
        def _(dve):
            links = [0]

            def link(ins):
                links[0] += 1
                ins.then_inc(Q["dve_link"], 1)
                dve.wait_ge(Q["dve_link"], links[0])

            def rsqrt(y, var, n, P=128):
                v, a, g = rs_v[0:P, 0:n], rs_a[0:P, 0:n], rs_g[0:P, 0:n]
                link(dve.tensor_scalar(v, var, EPS, None, ALU.add))
                link(dve.tensor_scalar(g.bitcast(I32), v.bitcast(I32), -0.5, float(0x5F3759DF), ALU.mult, ALU.add))
                for k in range(3):
                    link(dve.tensor_tensor(a, g, g, ALU.mult))
                    link(dve.scalar_tensor_tensor(out=a, in0=a, scalar=-0.5, in1=v, op0=ALU.mult, op1=ALU.mult))
                    link(dve.scalar_tensor_tensor(out=(y if k == 2 else g), in0=a, scalar=1.5, in1=g, op0=ALU.add, op1=ALU.mult))

            def layer_norm(dst, src, n, done, P=128, twice=False):
                for i in range(n):
                    ins = dve.bn_stats(stats[0:P, i, :], src[:, i, :])
                link(ins)
                for i in range(n):
                    ins = dve.bn_aggr(mv[0:P, i, :], stats[0:P, i, :])
                link(ins)
                rsqrt(rstd[0:P, 0:n], mv[0:P, 0:n, 1], n, P)
                if twice:
                    s1, s2, v2 = rstd[0:P, 0:n], rs_w[0:P, 0:n], rs_x[0:P, 0:n]
                    link(dve.tensor_tensor(v2, s1, s1, ALU.mult))
                    link(dve.tensor_tensor(v2, v2, mv[0:P, 0:n, 1], ALU.mult))
                    rsqrt(s2, v2, n, P)
                    link(dve.tensor_tensor(s1, s1, s2, ALU.mult))
                for i in range(n):
                    ins = dve.tensor_scalar(dst[:, i, :], src[:, i, :], mv[0:P, i, 0:1], rstd[0:P, i:i + 1],
                                            ALU.subtract, ALU.mult)
                    if done is not None:
                        ins.then_inc(done, 1)
                if done is None:
                    link(ins)

            dve.wait_ge(ld_x, 16)
            layer_norm(xn_tok, x_tok, NT, xn_done)
            dve.wait_ge(ld_w, 16 * 5)
            dve.tensor_copy(v_rep[:], v_col[:].to_broadcast([D, D])).then_inc(halves_done, 1)
            dve.tensor_scalar(wi[:, :, 0:2 * D], wi[:, :, 0:2 * D], 0.5, None, ALU.mult).then_inc(halves_done, 1)
            dve.tensor_scalar(uh[:], uh[:], 0.5, None, ALU.mult).then_inc(halves_done, 1)
            dve.tensor_scalar(b_col[:, 0:2], b_col[:, 0:2], 0.5, None, ALU.mult).then_inc(halves_done, 1)
            dve.wait_ge(halves_done, 4)
            dve.tensor_copy(uh_part[:, 0, :], uh[:]).then_inc(uparts_done, 1)
            dve.wait_ge(uparts_done, 1)
            dve.tensor_tensor(uh_rest[:], uh[:], uh_part[:, 0, :], ALU.subtract).then_inc(uparts_done, 1)
            dve.wait_ge(uparts_done, 2)
            dve.tensor_copy(uh_part[:, 1, :], uh_rest[:]).then_inc(uparts_done, 1)
            dve.wait_ge(uparts_done, 3)
            dve.tensor_tensor(uh_part[:, 2, :], uh_rest[:], uh_part[:, 1, :], ALU.subtract).then_inc(uparts_done, 1)
            dve.wait_ge(setup_pe, 1)
            dve.tensor_copy(encT[:].rearrange("p b s -> p (b s)"), bank[6][:, 0:B * S]).then_inc(setup_ev, 1)
            for b in range(B):
                dve.wait_ge(setup_pe, 2 + b)
                dve.tensor_copy(xnT[:, b, :], bank[b][:, :]).then_inc(setup_ev, 1)
            for g in range(3):
                dve.wait_ge(setup_pe, 4 + g)
                dve.tensor_copy(ewx[:, :, g, 0:S], bank[2 + g][:, 0:B * S].rearrange("p (b s) -> p b s", b=B)).then_inc(setup_ev, 1)

            for b in range(B):
                for g in range(3):
                    dve.wait_ge(setup_pe, 7 + b * 3 + g)
                    dve.tensor_scalar(xg[:, b, :, g], bank[(6, 7, 0, 1, 5, 6)[b * 3 + g]][:], b_col[:, g:g + 1], None, ALU.add).then_inc(setup_ev, 1)

            dve.wait_ge(Q["ld_slot"], 16)
            layer_norm(slot_nrm, slot_tok, NJ, Q["pre_ev"])
            dve.wait_ge(ld_ctx, 16)
            layer_norm(ctxn, ctx_tok, B * NCC, Q["pre_ev"], P=CP)
            dve.wait_ge(Q["ld_cols"], 16 * 15)
            link(dve.tensor_scalar(cols[:, 0:2], cols[:, 0:2], scale_col, None, ALU.mult))
            for h in range(2):
                dve.wait_ge(Q["pre_tr"], 1 + h)
                dve.tensor_scalar(seT[:, h * 512:(h + 1) * 512], bank[h], sg_col, sbias_col, ALU.mult, ALU.add).then_inc(Q["pre_ev"], 1)
            dve.wait_ge(Q["pre_tr"], 3)
            dve.tensor_scalar(ctxnT[:], bank[2][:, 0:B * S], kvg_col, kvb_col, ALU.mult, ALU.add).then_inc(Q["pre_ev"], 1)
            dve.wait_ge(Q["pre_tr"], 4)
            dve.tensor_scalar(kT[:], bank[3][:, 0:B * S], bk_col, None, ALU.add).then_inc(Q["pre_ev"], 1)
            dve.wait_ge(Q["pre_tr"], 5)
            dve.tensor_scalar(vT[:], bank[4][:, 0:B * S], bv_col, None, ALU.add).then_inc(Q["pre_ev"], 1)
            dve.wait_ge(Q["ld_rep"], 16 * 8)
            dve.wait_ge(Q["pre_tr"], 6)
            dve.tensor_tensor(vw[:, :, 0:D], bank[5][0:CP, :].rearrange("p (i d) -> p i d", i=B * NCC),
                              bu_rep[:].unsqueeze(1).to_broadcast([CP, B * NCC, D]), ALU.add).then_inc(Q["pre_ev"], 1)
            dve.wait_ge(Q["pre_tr"], 7)
            dve.tensor_copy(sh_turned[:, 0:2, :], bank[6].rearrange("p (c f) -> p c f", c=2)).then_inc(Q["pre_ev"], 1)
            dve.tensor_copy(sh_turned[:, 2, :], bank[7][:, 0:F]).then_inc(Q["pre_ev"], 1)
            dve.tensor_tensor(cls_rep[:], cls_rep[:], b2_rep[:].unsqueeze(1).to_broadcast([128, B, D]), ALU.add).then_inc(Q["pre_ev"], 1)
            dve.wait_ge(consts_done, 3)
            dve.tensor_copy(sel[:], ident[0:E1, 0:E1].unsqueeze(2).to_broadcast([E1, E1, 128])).then_inc(Q["pre_ev"], 1)

            def columns(b, t, s):
                dve.wait_ge(gates_done[b], t + 1)
                dve.tensor_reduce(ewx[:, b, :, S:S + 1].rearrange("p g o -> p (g o)"), gat[b][:, s, :, :], AX.X, ALU.add).then_inc(cols_done[b], 1)

            def row_max(b, t):
                dve.wait_ge(scores_done[b], t + 1)
                dve.tensor_reduce(nmax[:, b:b + 1], sco[b], AX.X, ALU.max, negate=True).then_inc(nmax_done[b], 1)

            def attend(b, t):
                dve.wait_ge(exp_done[b], t + 1)
                dve.reciprocal(rden[:, b:b + 1], probs[:, b, S:S + 1]).then_inc(rden_done[b], 1)
                dve.wait_ge(cols_done[b], t + 1)
                for g in (GZ, GR):
                    ins = dve.tensor_tensor_reduce(junk[:, b, g, :], probs[:, b, :], ewx[:, b, g, :], 1.0, 0.0, ALU.mult, ALU.add,
                                                   acc[b][:, g:g + 1])
                ins.then_inc(acc_zr[b], 1)
                dve.wait_ge(rden_done[b], t + 1)
                dve.tensor_tensor_reduce(junk[:, b, GH, :], probs[:, b, :], ewx[:, b, GH, :], rden[:, b:b + 1], 0.0, ALU.mult, ALU.add,
                                         base_h[:, b:b + 1]).then_inc(base_done[b], 1)

            def keep(b, t, s):
                dve.wait_ge(tzr_done[b], t + 1)
                dve.tensor_scalar(omz[:, b:b + 1], tzr[:, b, 0:1], -0.5, 0.5, ALU.mult, ALU.add).then_inc(omz_done[b], 1)
                dve.wait_ge(omz_done[b], t + 1)
                p = (s - 1) % U
                dve.scalar_tensor_tensor(out=nzh[:, b:b + 1], in0=omz[:, b:b + 1], scalar=hring[:, b, p:p + 1],
                                         in1=hring[:, b, p:p + 1], op0=ALU.mult, op1=ALU.subtract).then_inc(nzh_done[b], 1)

            def new_state(b, t, s):
                p = (s - 1) % U
                dve.wait_ge(cand_done[b], t + 1)
                dve.wait_ge(nzh_done[b], t + 1)
                if s == 0:
                    if not (isinstance(t, int) and t == 0):
                        dve.wait_ge(hist_saved[b], t)
                dve.scalar_tensor_tensor(out=hring[:, b, s:s + 1], in0=hcand[b], scalar=omz[:, b:b + 1],
                                         in1=nzh[:, b:b + 1], op0=ALU.mult, op1=ALU.subtract).then_inc(h_done[b], 1)

            def block_of_steps(t0, first=False):
                for s in range(U):
                    t = t0 + s
                    q = (s - 1) % U
                    if not (first and s == 0):
                        attend(1, t - 1)
                        keep(1, t - 1, q)
                    row_max(0, t)
                    if not (first and s == 0):
                        new_state(1, t - 1, q)
                    columns(0, t, s)
                    attend(0, t)
                    keep(0, t, s)
                    row_max(1, t)
                    new_state(0, t, s)
                    columns(1, t, s)

            dve.wait_ge(ld_h0, 16)
            block_of_steps(0, True)
            with dve.Fori(1, T // U) as k:
                block_of_steps(k * U)
            attend(1, T - 1)
            keep(1, T - 1, U - 1)
            new_state(1, T - 1, U - 1)

            for b in range(B):
                dve.wait_ge(Q["tr_b"], b + 1)
                ins = dve.tensor_tensor(x1[:, 4 * b:4 * b + 4, :], x_tok[:, 4 * b:4 * b + 4, :],
                                        bank[6 + b].rearrange("p (t d) -> p t d", t=4), ALU.add)
            link(ins)
            layer_norm(xB, x1, NT, Q["xB_done"], twice=True)
            for b in range(B):
                dve.wait_ge(Q["tr_b"], 3 + b)
                dve.tensor_scalar(xBT[:, b, :], bank[b], ng_col, nb_col, ALU.mult, ALU.add).then_inc(Q["xBT_done"], 1)

            def d_max(k):
                dve.wait_ge(Q["lt_done"], k + 1)
                dve.tensor_reduce(dmax[:, k:k + 1], bank[k % 2], AX.X, ALU.max, negate=True).then_inc(Q["dmax_done"], 1)

            def d_norm(k):
                dve.wait_ge(Q["dexp_done"], k + 1)
                link(dve.reciprocal(drec[:, k:k + 1], dsum[:, k:k + 1]))
                dve.tensor_scalar(eD[:, k % 3, :], eD[:, k % 3, :], drec[:, k:k + 1], None, ALU.mult).then_inc(Q["dnorm_done"], 1)

            def d_slots(k):
                b, j = k // NJ, k % NJ
                dve.wait_ge(Q["ds_done"], k + 1)
                dve.tensor_scalar(slotsT[:, 2 * j:2 * j + 2, b, :], bank[4 + k % 2][:, 0:128].rearrange("p (e s) -> p e s", e=2),
                                  ng_col, nb_col, ALU.mult, ALU.add).then_inc(Q["slots_ev"], 1)

            for k in range(16 + 3):
                if k < 16:
                    d_max(k)
                if 1 <= k <= 16:
                    d_norm(k - 1)
                if k >= 3:
                    d_slots(k - 3)

            def c_max(m):
                p = (6, 0)[m % 2]
                dve.wait_ge(Q["l_done"], m + 1)
                dve.tensor_reduce(cmax[:, m:m + 1], psum[:, p:p + 2, :], AX.XY, ALU.max, negate=True).then_inc(Q["cmax_done"], 1)

            def c_copy(m):
                b, i = m // 4, m % 4
                dve.wait_ge(Q["ctr_done"], m + 1)
                dve.tensor_copy(eCT[:, b, 4:8, i * 128:(i + 1) * 128],
                                bank[3 + 2 * (m % 2)].rearrange("p (j n) -> p j n", j=4)).then_inc(Q["cT_dve"], 1)

            for m in range(8 + 1):
                if m < 8:
                    c_max(m)
                if m >= 1:
                    c_copy(m - 1)
            dve.wait_ge(Q["cexp_done"], 8)
            link(dve.reciprocal(crec[:], csum[:]))

            def expert_bias(j):
                dve.wait_ge(Q["eo_mm"], 2 * j + 2)
                dve.tensor_tensor(eo[:, j, :, :], bank[4 + j % 2][:, 0:B * D].rearrange("p (b d) -> p b d", b=B),
                                  bd_rep[:, j, :].unsqueeze(1).to_broadcast([128, B, D]), ALU.add).then_inc(Q["eo_ev"], 1)

            dve.wait_ge(Q["ld_exp"], 16 * 7)
            for e in range(E0):
                dve.wait_ge(Q["egelu"], e + 1)
                if e >= 2:
                    dve.wait_ge(Q["eo_mm"], e - 1)
                for f in range(FC):
                    ins = dve.scalar_tensor_tensor(out=gu[:, e % 2, f, :], in0=bank[2 + e % 2][:, f * 128:(f + 1) * 128],
                                                   scalar=bu_col[:, e * FC + f:e * FC + f + 1], in1=ga[:, e % 2, f, :],
                                                   op0=ALU.add, op1=ALU.mult)
                ins.then_inc(Q["egu"], 1)
                if e >= 2 and e % 2 == 0:
                    expert_bias(e // 2 - 1)
            expert_bias(NJ - 1)
            for m in range(NT):
                dve.wait_ge(Q["cm_mm"], m + 1)
                dve.scalar_tensor_tensor(out=x2[:, m, :], in0=bank[6 + m % 2][:, 0:D], scalar=crec[:, m:m + 1], in1=x1[:, m, :],
                                         op0=ALU.mult, op1=ALU.add).then_inc(Q["x2_done"], 1)
            dve.wait_ge(Q["x2_done"], NT)

            layer_norm(lnt, x2, NT, None)
            dve.wait_ge(Q["sig_done"], 1)
            link(dve.tensor_tensor(slots, lnt, sig_rep[:].unsqueeze(1).to_broadcast([128, NT, D]), ALU.mult))
            link(dve.tensor_tensor(slots, slots, mu_rep[:].unsqueeze(1).to_broadcast([128, NT, D]), ALU.add))
            for it in range(ITERS):
                for b in range(B):
                    layer_norm(lnt[:, 4 * b:4 * b + 4, :], slots[:, 4 * b:4 * b + 4, :], 4, CQ["q_ln"][b])
                for b in range(B):
                    dve.wait_ge(CQ["log_mm"][b], it + 1)
                    link(dve.tensor_reduce(amax[:, b, :], psum[0:CP, 4 * b + 2:4 * b + 4, :], AX.X, ALU.max, negate=True))
                    dve.tensor_scalar(amax[:, b, :], amax[:, b, :], QK_SCALE, None, ALU.mult).then_inc(CQ["amax"][b], 1)
                for b in range(B):
                    dve.wait_ge(CQ["exp"][b], it + 1)
                    link(dve.reciprocal(arec[:, b, :], asum[:, b, :]))
                    for c in range(NCC):
                        ins = dve.tensor_scalar(attn[:, b, c, :], attn[:, b, c, :], arec[:, b, c:c + 1], EPS_ATTN, ALU.mult, ALU.add)
                    ins.then_inc(CQ["attn"][b], 1)
                for b in range(B):
                    dve.wait_ge(CQ["upd_mm"][b], it + 1)
                    upd = psum[:, 4 * b:4 * b + 2, 0:2 * (D + 1)].rearrange("p a (k d) -> p a k d", k=2)
                    link(dve.reciprocal(urec[:, b, :].rearrange("p (a k) -> p a k", k=2), upd[:, :, :, D]))
                    for k in range(4):
                        ins = dve.scalar_tensor_tensor(out=slots[:, 4 * b + k, :], in0=upd[:, k // 2, k % 2, 0:D],
                                                       scalar=urec[:, b, k:k + 1], in1=slots[:, 4 * b + k, :],
                                                       op0=ALU.mult, op1=ALU.add)
                    link(ins)
                    layer_norm(lnt[:, 4 * b:4 * b + 4, :], slots[:, 4 * b:4 * b + 4, :], 4, CQ["m_ln"][b])
                for b in range(B):
                    sl = slots[:, 4 * b:4 * b + 4, :]
                    ln = lnt[:, 4 * b:4 * b + 4, :]
                    dve.wait_ge(CQ["w2_mm"][b], it + 1)
                    link(dve.tensor_tensor(sl, sl, bank[4 * b].rearrange("p (k d) -> p k d", k=4), ALU.add))
                    link(dve.tensor_tensor(sl, sl, cls_rep[:, b, :].unsqueeze(1).to_broadcast([128, 4, D]), ALU.add))
                    layer_norm(ln, sl, 4, None)
                    link(dve.tensor_tensor(ln, ln, pg_rep[:].unsqueeze(1).to_broadcast([128, 4, D]), ALU.mult))
                    link(dve.tensor_tensor(sl, ln, pb_rep[:].unsqueeze(1).to_broadcast([128, 4, D]), ALU.add))
            link(dve.tensor_tensor(x3, x2, slots, ALU.add))

            layer_norm(lnt, x3, NT, Q["yn_done"])
            dve.wait_ge(Q["r_mm"], 1)
            dve.wait_ge(Q["gates_done_d"], 1)
            link(dve.tensor_copy(sc[:].rearrange("p t e -> p (t e)"), bank[2][:, 0:NT * E1]))
            link(dve.tensor_scalar(gates[:], gates[:], 1.0, None, ALU.add))
            link(dve.reciprocal(gates[:], gates[:]))
            link(dve.memset(rank[:], 0.0))
            for j in range(E1):
                if j + 1 < E1:
                    ins = dve.tensor_tensor(beats[:, :, j + 1:], sc[:, :, j:j + 1].to_broadcast([128, NT, E1 - 1 - j]), sc[:, :, j + 1:], ALU.is_ge)
                if j:
                    ins = dve.tensor_tensor(beats[:, :, 0:j], sc[:, :, j:j + 1].to_broadcast([128, NT, j]), sc[:, :, 0:j], ALU.is_gt)
                link(ins)
                if j + 1 < E1:
                    ins = dve.tensor_tensor(rank[:, :, j + 1:], rank[:, :, j + 1:], beats[:, :, j + 1:], ALU.add)
                if j:
                    ins = dve.tensor_tensor(rank[:, :, 0:j], rank[:, :, 0:j], beats[:, :, 0:j], ALU.add)
                link(ins)
            dve.scalar_tensor_tensor(out=gates[:], in0=rank[:], scalar=float(TOP_K), in1=gates[:], op0=ALU.is_lt, op1=ALU.mult)\
               .then_inc(Q["gates_done_d"], 1)
            for b in range(B):
                dve.wait_ge(Q["tr_g"], b + 1)
                dve.tensor_copy(gTr[:, b, :], bank[4 + b][0:E1, :]).then_inc(Q["gTr_done"], 1)

            def route(q):
                if q >= B:
                    dve.wait_ge(Q["rep_mm"], q + 1 - B)
                    if q >= B + 2:
                        dve.wait_ge(Q["m_mm"], 2 * (q - 1))
                    dve.tensor_tensor(routed[:, q % 2, :], yT[:, q % B, :], bank[4 + q % 2], ALU.mult).then_inc(Q["routed_done"], 1)

            def gated(u):
                dve.wait_ge(Q["silu_done"], u + 1)
                if u >= 2:
                    dve.wait_ge(Q["o_mm"], u - 1)
                dve.tensor_tensor(hT[:, u % 2, :], sil[:, u % 2, :], bank[2 + u % 2], ALU.mult).then_inc(Q["h_done_d"], 1)

            dve.wait_ge(Q["yT_done"], 2)
            for q in range(B * (E1 + 1)):
                if q + 1 < B * (E1 + 1):
                    route(q + 1)
                gated(2 * q)
                gated(2 * q + 1)
            for b in range(B):
                dve.wait_ge(Q["tr_o"], b + 1)
                dve.tensor_tensor(res[:, 4 * b:4 * b + 4, :], x3[:, 4 * b:4 * b + 4, :], bank[b].rearrange("p (t d) -> p t d", t=4),
                                  ALU.add).then_inc(Q["res_done"], 1)

        @block.tensor
        def _(pe):
            pe.wait_ge(consts_done, 6)
            pe.wait_ge(ld_ctx, 16)
            for i in range(B * NCC):
                ins = pe.transpose(bank[6][:, i * CP:(i + 1) * CP], ctx_tok[:, i, :], ident[0:CP, 0:CP])
            ins.then_inc(setup_pe, 1)
            for i in range(NT):
                pe.wait_ge(xn_done, i + 1)
                ins = pe.transpose(bank[i // 4][:, (i % 4) * 128:(i % 4 + 1) * 128], xn_tok[:, i, :], ident[:])
                if i % 4 == 3:
                    ins.then_inc(setup_pe, 1)
            pe.wait_ge(halves_done, 4)
            pe.wait_ge(setup_ev, 1)
            pe.wait_ge(setup_ev, 3)
            for g in range(3):
                pe.matmul(bank[2 + g][:, 0:B * S], wi[:, 1, g * D:(g + 1) * D], encT[:].rearrange("p b s -> p (b s)"),
                          start=True, stop=True).then_inc(setup_pe, 1)

            for b in range(B):
                for g in range(3):
                    i = b * 3 + g
                    pe.wait_ge(setup_ev, (1, 1, 3, 3, 6, 7)[i])
                    pe.matmul(bank[(6, 7, 0, 1, 5, 6)[i]][:], wi[:, 0, g * D:(g + 1) * D], xnT[:, b, :],
                              start=True, stop=True).then_inc(setup_pe, 1)

            pe.wait_ge(setup_ev, 12)
            for i in range(NJ):
                pe.wait_ge(Q["pre_ev"], i + 1)
                ins = pe.transpose(bank[i // 4][:, (i % 4) * 128:(i % 4 + 1) * 128], slot_nrm[:, i, :], ident[:])
                if i % 4 == 3:
                    ins.then_inc(Q["pre_tr"], 1)
            for i in range(B * NCC):
                pe.wait_ge(Q["pre_ev"], NJ + i + 1)
                ins = pe.transpose(bank[2][:, i * CP:(i + 1) * CP], ctxn[:, i, :], ident[0:CP, 0:CP])
            ins.then_inc(Q["pre_tr"], 1)
            pe.wait_ge(Q["ld_c"], 16 * 6)
            pe.wait_ge(Q["pre_ev"], 15)
            pe.matmul(bank[3][:, 0:B * S], wk[:], ctxnT[:], start=True, stop=True).then_inc(Q["pre_tr"], 1)
            pe.matmul(bank[4][:, 0:B * S], wv[:], ctxnT[:], start=True, stop=True).then_inc(Q["pre_tr"], 1)
            pe.wait_ge(Q["pre_ev"], 17)
            for i in range(B * NCC):
                ins = pe.matmul(bank[5][0:CP, i * D:(i + 1) * D], vT[:, i * CP:(i + 1) * CP], wus[:], start=True, stop=True)
            ins.then_inc(Q["pre_tr"], 1)
            pe.wait_ge(Q["ld_d"], 16 * 4)
            for c in range(FC):
                pe.transpose(bank[6][:, c * 128:(c + 1) * 128], sh_in[:, c, :], ident[:])
                pe.transpose(bank[6][:, F + c * 128:F + (c + 1) * 128], sh_sw[:, c, :], ident[:])
                ins = pe.transpose(bank[7][:, c * 128:(c + 1) * 128], sh_out[:, c * 128:(c + 1) * 128], ident[:])
            ins.then_inc(Q["pre_tr"], 1)
            pe.wait_ge(Q["pre_ev"], 22)

            def refresh(b, t):
                if not (isinstance(t, int) and t == 0):
                    pe.wait_ge(tanh_done[b], t)
                pe.matmul(pre[b], w_att[:, 1, :], encT[:, b, :], start=True, stop=False, skip_group_check=True)

            def x_part(b, t):
                pe.wait_ge(xblk_ready[b], t + U)
                pe.matmul(gat[b].rearrange("p s g i -> p (s g i)"), ident[:], xblk[:, b].rearrange("p s g i -> p (s g i)"), start=True, stop=False,
                          skip_group_check=True).then_inc(x_part_done[b], U)

            def keep_clock(n):
                for _ in range(n):
                    pe.matmul(bank[6], uh_part[:, 0, 0:D], uh_part[:].rearrange("p i m -> p (i m)")[:, 0:512], start=True, stop=True)

            def query(b, t, s):
                p = (s - 1) % U
                if isinstance(t, int) and t == 0:
                    pe.wait_ge(ld_h0, 16)
                else:
                    pe.wait_ge(h_done[b], t)
                pe.matmul(pre[b], w_att[:, 0, :], hring[:, b, p:p + 1].to_broadcast([D, S]), start=False, stop=True,
                          skip_group_check=True).then_inc(pre_done[b], 1)

            def h_gates(b, t, s):
                pe.wait_ge(part2[b], t + 1)
                for c, g in ((GZ, 0), (GR, 1), (GH, 2), (RH, 2)):
                    for i in range(3):
                        ins = pe.matmul(gat[b][:, s, c, i:3], uh_part[:, i, g * D:(g + 1) * D], h_part[:, b, 0:3 - i],
                                        start=False, stop=True, skip_group_check=True)
                ins.then_inc(gates_done[b], 1)

            def scores(b, t):
                pe.wait_ge(tanh_done[b], t + 1)
                pe.matmul(sco[b], v_rep[:], tanhT[:, b, :], start=True, stop=True).then_inc(scores_done[b], 1)

            def block_of_steps(t0, first=False, last=False):
                for s in range(U):
                    t = t0 + s
                    query(0, t, s)
                    refresh(1, t)
                    scores(0, t)
                    if s == 0:
                        x_part(0, t)
                    h_gates(0, t, s)
                    keep_clock(1)
                    query(1, t, s)
                    if not (last and s == U - 1):
                        refresh(0, t + 1)
                    scores(1, t)
                    if s == 0:
                        x_part(1, t)
                    h_gates(1, t, s)
                    keep_clock(1)

            pe.wait_ge(setup_ev, 12)
            pe.wait_ge(uparts_done, 4)
            pe.wait_ge(consts_done, 6)
            keep_clock(24)
            refresh(0, 0)
            block_of_steps(0, first=True)
            with pe.Fori(1, T // U - 1) as k:
                block_of_steps(k * U)
            block_of_steps(T - U, last=True)

            def turn(dst, tiles, done=None, step=None):
                for i, tile in enumerate(tiles):
                    if done is not None:
                        pe.wait_ge(done, step + i + 1)
                    ins = pe.transpose(dst[:, i * 128:(i + 1) * 128], tile, ident[:])
                return ins

            for b in range(B):
                pe.wait_ge(hist_saved[b], T)
                turn(bank[6 + b], [hist[:, b, i * 128:(i + 1) * 128] for i in range(4)]).then_inc(Q["tr_b"], 1)
            for b in range(B):
                turn(bank[b], [xB[:, 4 * b + i, :] for i in range(4)], Q["xB_done"], 4 * b).then_inc(Q["tr_b"], 1)

            def d_logits(k):
                b, j = k // NJ, k % NJ
                pe.wait_ge(Q["xBT_done"], b + 1 if k >= 2 else 2)
                if k >= 2:
                    pe.wait_ge(Q["dexp_done"], k - 1)
                pe.matmul(bank[k % 2], seT[:, j * 128:(j + 1) * 128], xBT[:, b, :], start=True, stop=True).then_inc(Q["lt_done"], 1)

            def d_turn(k):
                pe.wait_ge(Q["dnorm_done"], k + 1)
                if k >= 2:
                    pe.wait_ge(Q["dT_done"], k - 1)
                turn(bank[2 + k % 2], [eD[:, k % 3, i * 128:(i + 1) * 128] for i in range(4)]).then_inc(Q["dtr_done"], 1)

            def d_slots(k):
                b = k // NJ
                pe.wait_ge(Q["dT_done"], k + 1)
                if k >= 2:
                    pe.wait_ge(Q["slots_ev"], k - 1)
                for i in range(4):
                    ins = pe.matmul(bank[4 + k % 2][:, 0:128], xB[:, 4 * b + i, :], dT[:, k % 2, i * 128:(i + 1) * 128],
                                    start=(i == 0), stop=(i == 3))
                ins.then_inc(Q["ds_done"], 1)

            for k in range(16 + 2):
                if k < 16:
                    d_logits(k)
                if 1 <= k <= 16:
                    d_turn(k - 1)
                if k >= 2:
                    d_slots(k - 2)

            def c_logits(m):
                b, i = m // 4, m % 4
                p = (6, 0)[m % 2]
                if m == 1:
                    pe.wait_ge(Q["dexp_done"], 16)
                if m >= 2:
                    pe.wait_ge(Q["cexp_done"], m - 1)
                for h in range(2):
                    ins = pe.matmul(bank[p + h], xBT[:, b, i * 128:(i + 1) * 128], seT[:, h * 512:(h + 1) * 512], start=True, stop=True)
                ins.then_inc(Q["l_done"], 1)

            def c_turn(m):
                pe.wait_ge(Q["cexp_done"], m + 1)
                if m == 0:
                    pe.wait_ge(Q["dT_done"], 16)
                if m == 1:
                    pe.wait_ge(Q["slots_ev"], 16)
                if m >= 2:
                    pe.wait_ge(Q["cT_act"], m - 1)
                    pe.wait_ge(Q["cT_dve"], m - 1)
                for h in range(2):
                    ins = turn(bank[2 + 2 * (m % 2) + h], [eC[:, m % 2, (4 * h + i) * 128:(4 * h + i + 1) * 128] for i in range(4)])
                ins.then_inc(Q["ctr_done"], 1)

            for m in range(8 + 1):
                if m < 8:
                    c_logits(m)
                if m >= 1:
                    c_turn(m - 1)

            def e_in(e):
                if e == 0:
                    pe.wait_ge(Q["ld_exp"], 16 * 7)
                    pe.wait_ge(Q["slots_ev"], 16)
                    pe.wait_ge(Q["cexp_done"], 8)
                    pe.wait_ge(Q["cT_act"], 8)
                    pe.wait_ge(Q["cT_dve"], 8)
                if e >= 2:
                    pe.wait_ge(Q["egelu"], e - 1)
                    pe.wait_ge(Q["egu"], e - 1)
                x = slotsT[:, e].rearrange("p b s -> p (b s)")
                for f in range(FC):
                    pe.matmul(bank[e % 2][:, f * 128:(f + 1) * 128], wg[:, e, f * 128:(f + 1) * 128], x, start=True, stop=True)
                    ins = pe.matmul(bank[2 + e % 2][:, f * 128:(f + 1) * 128], wu_[:, e, f * 128:(f + 1) * 128], x, start=True, stop=True)
                ins.then_inc(Q["e_mm"], 1)

            def e_out(e):
                j, r = e // 2, 64 * (e % 2)
                pe.wait_ge(Q["egu"], e + 1)
                if j >= 2:
                    pe.wait_ge(Q["eo_ev"], j - 1)
                for b in range(B):
                    for f in range(FC):
                        ins = pe.matmul(bank[4 + j % 2][r:r + 64, b * D:(b + 1) * D], gu[:, e % 2, f, b * SL0:(b + 1) * SL0],
                                        wd[:, e * FC + f, :], start=(f == 0), stop=(f == FC - 1), skip_group_check=True)
                ins.then_inc(Q["eo_mm"], 1)

            for e in range(E0 + 1):
                if e < E0:
                    e_in(e)
                if e >= 1:
                    e_out(e - 1)
            pe.wait_ge(Q["eo_ev"], NJ)
            for m in range(NT):
                b, i = m // 4, m % 4
                if m >= 2:
                    pe.wait_ge(Q["x2_done"], m - 1)
                for j in range(NJ):
                    ins = pe.matmul(bank[6 + m % 2][:, 0:D], eCT[:, b, j, i * 128:(i + 1) * 128], eo[:, j, b, :],
                                    start=(j == 0), stop=(j == NJ - 1))
                ins.then_inc(Q["cm_mm"], 1)

            for it in range(ITERS):
                for b in range(B):
                    turn(bank[4 * b], [lnt[:, 4 * b + i, :] for i in range(4)], CQ["q_ln"][b], 4 * it).then_inc(CQ["q_tr"][b], 1)
                for b in range(B):
                    pe.wait_ge(CQ["q_lnT"][b], it + 1)
                    pe.matmul(bank[4 * b + 1], wq[:], lnT[:, b, :], start=True, stop=True).then_inc(CQ["q_mm"][b], 1)
                for b in range(B):
                    pe.wait_ge(CQ["q_T"][b], it + 1)
                    for c in range(NCC):
                        ins = pe.matmul(bank[4 * b + 2 + c][0:CP, :], kT[:, (b * NCC + c) * CP:(b * NCC + c + 1) * CP], qT[:, b, :],
                                        start=True, stop=True)
                    ins.then_inc(CQ["log_mm"][b], 1)
                for b in range(B):
                    pe.wait_ge(CQ["attn"][b], it + 1)
                    for k in range(4):
                        for c in range(NCC):
                            ins = pe.matmul(bank[4 * b + k // 2][:, (k % 2) * (D + 1):(k % 2 + 1) * (D + 1)],
                                            attn[:, b, c, k * 128:(k + 1) * 128], vw[:, b * NCC + c, :],
                                            start=(c == 0), stop=(c == NCC - 1))
                    ins.then_inc(CQ["upd_mm"][b], 1)
                for b in range(B):
                    turn(bank[4 * b + 2], [lnt[:, 4 * b + i, :] for i in range(4)], CQ["m_ln"][b], 4 * it).then_inc(CQ["m_tr"][b], 1)
                for b in range(B):
                    pe.wait_ge(CQ["m_lnT"][b], it + 1)
                    pe.matmul(bank[4 * b + 3], w1[:], lnT[:, b, :], start=True, stop=True).then_inc(CQ["m_mm"][b], 1)
                for b in range(B):
                    pe.wait_ge(CQ["gelu"][b], it + 1)
                    for k in range(4):
                        ins = pe.matmul(bank[4 * b][:, k * 128:(k + 1) * 128], gT[:, b, k * 128:(k + 1) * 128], w2[:],
                                        start=True, stop=True)
                    ins.then_inc(CQ["w2_mm"][b], 1)

            for b in range(B):
                turn(bank[b], [lnt[:, 4 * b + i, :] for i in range(4)], Q["yn_done"], 4 * b).then_inc(Q["tr_y"], 1)
            pe.wait_ge(Q["yT_done"], 2)
            for i in range(NT):
                ins = pe.matmul(bank[2][:, i * E1:(i + 1) * E1], yT[:, i // 4, (i % 4) * 128:(i % 4 + 1) * 128], router[:],
                                start=True, stop=True)
            ins.then_inc(Q["r_mm"], 1)
            pe.wait_ge(Q["gates_done_d"], 2)
            for i in range(NT):
                ins = pe.transpose(bank[4 + i // 4][0:E1, (i % 4) * 128:(i % 4 + 1) * 128], gates[:, i, :], ident[:])
                if i % 4 == 3:
                    ins.then_inc(Q["tr_g"], 1)
            pe.wait_ge(Q["gTr_done"], 2)
            order = [E1] + list(range(E1))

            def replicate(q):
                if q >= B + 2:
                    pe.wait_ge(Q["routed_done"], q - 1 - B)
                pe.matmul(bank[4 + q % 2], sel[:, order[q // B], :], gTr[:, q % B, :], start=True, stop=True).then_inc(Q["rep_mm"], 1)

            def d_in(u):
                q, f = u // 2, u % 2
                e = order[q // B]
                x = yT[:, q % B, :] if q < B else routed[:, q % 2, :]
                w_in, w_sw = (sh_turned[:, 0, :], sh_turned[:, 1, :]) if q < B else (win[:, e, :], wsw[:, e, :])
                if q >= B:
                    pe.wait_ge(Q["routed_done"], q + 1 - B)
                if q == B:
                    pe.wait_ge(Q["ld_moe"], 16 * 3)
                if u >= 2:
                    pe.wait_ge(Q["silu_done"], u - 1)
                    pe.wait_ge(Q["h_done_d"], u - 1)
                pe.matmul(bank[u % 2], w_in[:, f * 128:(f + 1) * 128], x, start=True, stop=True)
                pe.matmul(bank[2 + u % 2], w_sw[:, f * 128:(f + 1) * 128], x, start=True, stop=True).then_inc(Q["m_mm"], 1)

            def d_out(u):
                q, f = u // 2, u % 2
                e = order[q // B]
                pe.wait_ge(Q["h_done_d"], u + 1)
                w_o = sh_turned[:, 2, :] if q < B else wout[:, e, :]
                pe.matmul(bank[6 + q % B], w_o[:, f * 128:(f + 1) * 128], hT[:, u % 2, :], start=(q < B and f == 0),
                          stop=(q // B == E1 and f == 1), skip_group_check=True).then_inc(Q["o_mm"], 1)

            NU = 2 * B * (E1 + 1)
            for u in range(NU + 2):
                if u < NU:
                    if u % 2 == 0 and B <= u // 2 + 1 < B * (E1 + 1):
                        replicate(u // 2 + 1)
                    d_in(u)
                if u >= 2:
                    d_out(u - 2)
            for b in range(B):
                pe.wait_ge(Q["outT_done"], b + 1)
                turn(bank[b], [outT[:, b, i * 128:(i + 1) * 128] for i in range(4)]).then_inc(Q["tr_o"], 1)


def kernel(**inputs):
    import numpy as np
    import concourse.bacc as bacc
    from concourse import mybir as mb
    from concourse.bass_utils import run_bass_kernel_spmd as run
    nc = bacc.Bacc("TRN2", target_bir_lowering=False, num_devices=1)
    arrays, aps = {}, {}
    for name, a in inputs.items():
        a = np.ascontiguousarray(a)
        arrays[f"in_{name}"] = a
        aps[name] = nc.dram_tensor(f"in_{name}", a.shape, mb.dt.from_np(a.dtype), kind="ExternalInput").ap()
    out = nc.dram_tensor("out_0", (2, 512, 128), mb.dt.float32, kind="ExternalOutput").ap()
    build(nc, aps, out)
    r = run(nc, [arrays], core_ids=[0])
    return r.results[0]["out_0"]
```

```python
from contextlib import ExitStack

import concourse.bass as bass
from concourse import mybir

F32 = mybir.dt.float32
I32 = mybir.dt.int32
BF16 = mybir.dt.bfloat16
ALU = mybir.AluOpType
ACT = mybir.ActivationFunctionType
AX = mybir.AxisListType

B, T, D = 2, 512, 128
S = 154
NT = B * T // 128
NCC = 2
CP = S // NCC
U = 8
GZ, GR, GH, RH = range(4)
EPS = 1e-5
EPS_ATTN = 1e-8
E0, SL0, F = 16, 64, 256
NS = E0 * SL0
NJ = NS // 128
ITERS = 3
QK_SCALE = float(D) ** 0.5
E1 = 8
TOP_K = 2
FC = F // 128
N_CONSTS = 7
N_SETUP_EV = 12
PRE_CTXT, PRE_V, PRE_ALL = NJ + B * NCC + 3, NJ + B * NCC + 7, NJ + B * NCC + 10


def build(nc, A, out):
    with ExitStack() as ctx:
        def sb(name, shape, dt=F32):
            return ctx.enter_context(nc.sbuf_tensor(name, shape, dt))

        def sem(name):
            return ctx.enter_context(nc.semaphore(name))

        psum = ctx.enter_context(nc.psum_tensor("psum", [128, 8, 512], F32))
        bank = [psum[:, i, :] for i in range(8)]

        ident = sb("ident", [128, 128])
        zero_col = sb("zero_col", [128, 1])
        half_col = sb("half_col", [128, 1])
        x_tok = sb("x_tok", [128, NT, D])
        ctx_tok = sb("ctx_tok", [CP, B * NCC, D])
        w_att = sb("w_att", [D, 2, D])
        v_col = sb("v_col", [D, 1])
        v_rep = sb("v_rep", [D, D])
        wi = sb("wi", [D, 2, 3 * D])
        uh = sb("uh", [D, 3 * D])
        stats = sb("stats", [128, NT, 6])
        mv = sb("mv", [128, NT, 2])
        rstd = sb("rstd", [128, NT])
        turned = sb("turned", [128, 2, B * T])
        xnT, hist = (turned[:, i, :].rearrange("p (b t) -> p b t", b=B) for i in range(2))
        eC = turned
        encT = sb("encT", [128, B, S])
        ewx = sb("ewx", [128, B, 4, S + 1])
        hring = sb("hring", [128, B, U])
        xblk = sb("xblk", [128, B, U, 4, 3])
        xg = sb("xg", [128, B, T, 3])
        b_col = sb("b_col", [D, 3])
        uh_part = sb("uh_part", [D, 3, 3 * D], BF16)
        uh_rest = sb("uh_rest", [D, 3 * D])
        h_part = sb("h_part", [128, B, 3], BF16)
        h_rest = sb("h_rest", [128, B])
        tanhT = sb("tanhT", [128, B, S])
        probs = sb("probs", [128, B, S + 1])
        junk = sb("junk", [128, B, 3, S + 1])
        nmax = sb("nmax", [128, B])
        rden = sb("rden", [128, B])
        base_h = sb("base_h", [128, B])
        tzr = sb("tzr", [128, B, 2])
        omz = sb("omz", [128, B])
        zh = sb("zh", [128, B])
        half_h = sb("half_h", [128, B])

        seT = sb("seT", [128, NS])
        cols = sb("cols", [128, 16])
        sg_col, sbias_col, scale_col = cols[:, 0:1], cols[:, 1:2], cols[:, 2:3]
        ng_col, nb_col = cols[:, 3:4], cols[:, 4:5]
        kvg_col, kvb_col, bk_col, bv_col, bq_col, b1_col = (cols[:, i:i + 1] for i in range(5, 11))
        qg_col, qb_col, mg_col, mb_col = (cols[:, i:i + 1] for i in range(11, 15))
        x1 = sb("x1", [128, NT, D])
        xB = sb("xB", [128, NT, D])
        xBT = sb("xBT", [128, B, T])
        dmax, dsum, drec = sb("dmax", [128, 16]), sb("dsum", [128, 16]), sb("drec", [128, 16])
        slotsT = sb("slotsT", [128, E0, B, SL0])
        cmax, csum, crec = sb("cmax", [128, NT]), sb("csum", [128, NT]), sb("crec", [128, NT])
        eCT = sb("eCT", [128, B, NJ, T])
        wg, wu_ = sb("wg", [128, E0, F]), sb("wu_", [128, E0, F])
        wd = sb("wd", [128, E0 * FC, D])
        bg_col, bu_col = sb("bg_col", [128, E0 * FC]), sb("bu_col", [128, E0 * FC])
        bd_rep = sb("bd_rep", [128, NJ, D])
        ga, gu = sb("ga", [128, 2, FC, 128]), sb("gu", [128, 2, FC, 128])
        eo = sb("eo", [128, NJ, B, D])
        ctxn = sb("ctxn", [CP, B * NCC, D])
        ctxnT, kT, vT = sb("ctxnT", [128, B * S]), sb("kT", [128, B * S]), sb("vT", [128, B * S])
        wk, wv, wq, wus, w1, w2 = (sb(n, [128, D]) for n in ("wk", "wv", "wq", "wus", "w1", "w2"))
        bu_rep = sb("bu_rep", [CP, D])
        vw = sb("vw", [CP, B * NCC, D + 1])
        mu_rep, sig_rep = sb("mu_rep", [128, D]), sb("sig_rep", [128, D])
        cls_rep = sb("cls_rep", [128, B, D])
        b2_rep, pg_rep, pb_rep = sb("b2_rep", [128, D]), sb("pg_rep", [128, D]), sb("pb_rep", [128, D])
        late = eCT[:].rearrange("p b j t -> p (b j t)")
        wg_flat, wu_flat, wd_flat = (w[:].rearrange("p e f -> p (e f)") for w in (wg, wu_, wd))

        def tok_view(t, i):
            return t[:, i * NT * D:(i + 1) * NT * D].rearrange("p (t d) -> p t d", t=NT)

        def turned_view(t, i):
            return t[:, i * B * T:(i + 1) * B * T].rearrange("p (b t) -> p b t", b=B)

        lnt, x3 = tok_view(late, 0), tok_view(late, 6)
        moved = tok_view(wd_flat, 0)
        lnT, qT, gT, yT = (turned_view(late, i) for i in (1, 2, 3, 7))
        attn = late[0:CP, 4 * B * T:6 * B * T].rearrange("p (b c t) -> p b c t", b=B, c=NCC)
        amax, asum, arec = (sb(n, [CP, B, NCC]) for n in ("amax", "asum", "arec"))
        urec = sb("urec", [128, B, 4])
        router = sb("router", [128, E1])
        sh_turned = sb("sh_turned", [128, 3, F])
        slot_tok, slot_nrm, xn_tok, shared = (tok_view(late, i) for i in range(4))
        sh_in, sh_sw = shared[:, 0:FC, :], shared[:, FC:2 * FC, :]
        sh_out = shared[:, 2 * FC:3 * FC, :].rearrange("p c d -> p (c d)")
        slotsT_flat = slotsT[:].rearrange("p e b s -> p (e b s)")
        slots, x2 = tok_view(slotsT_flat, 0), tok_view(slotsT_flat, 1)
        sc, rank, beats, gates = (sb(n, [128, NT, E1]) for n in ("sc", "rank", "beats", "gates"))
        gate_part = sb("gate_part", [128, NT, 3, E1], BF16)
        gate_rest = sb("gate_rest", [128, NT, E1])
        gTr = sb("gTr", [3 * E1, B, T], BF16)
        sel = sb("sel", [3 * E1, E1, 128], BF16)
        sel_col = sb("sel_col", [3 * E1, E1])
        ident16 = sb("ident16", [128, 128], BF16)
        win = wg_flat[:, 0:E1 * F].rearrange("p (e f) -> p e f", e=E1)
        wsw = wg_flat[:, E1 * F:2 * E1 * F].rearrange("p (e f) -> p e f", e=E1)
        wout = wu_flat[:, 0:E1 * F].rearrange("p (e f) -> p e f", e=E1)
        routed, sil, hT, outT = (turned_view(wd_flat, i) for i in range(4))
        res = tok_view(wu_flat, 3)

        names = """ld_slot ld_cols ld_exp ld_c ld_rep ld_d dve_link pre_tr pre_ev sig_done
            tr_b xB_done xBT_done lt_done dmax_done dexp_done dnorm_done dtr_done dT_done ds_done slots_ev
            l_done cmax_done cexp_done ctr_done cT_act cT_dve e_mm egelu egu eo_mm eo_ev cm_mm x2_done
            yn_done tr_y yT_done r_mm gates_done_d tr_g gTr_done rep_mm routed_done m_mm silu_done h_done_d o_mm
            outT_done tr_o res_done ld_moe""".split()
        Q = {n: sem(n) for n in names}
        CQ = {n: [sem(f"c_{n}{b}") for b in range(B)] for n in
              "q_ln q_tr q_lnT q_mm q_T log_mm amax exp attn upd_mm m_ln m_tr m_lnT m_mm gelu w2_mm".split()}

        rs_v = sb("rs_v", [128, NT])
        minus_half = sb("minus_half", [128, NT])
        var_ready, rstd_ready = sem("var_ready"), sem("rstd_ready")
        centred = [sem(f"centred{b}") for b in range(B)]
        moved_done = [sem(f"moved_done{b}") for b in range(B)]
        xg_flat = xg[:].rearrange("p b t g -> p (b t g)")
        eD = xg_flat[:, 0:3 * T].rearrange("p (i t) -> p i t", i=3)
        dT = xg_flat[:, 3 * T:5 * T].rearrange("p (i t) -> p i t", i=2)

        ld_x, ld_ctx, ld_w, ld_h0 = sem("ld_x"), sem("ld_ctx"), sem("ld_w"), sem("ld_h0")
        consts_done = sem("consts_done")
        xn_done = sem("xn_done")
        halved = sem("halved")
        setup_pe, setup_ev = sem("setup_pe"), sem("setup_ev")
        out_done = sem("out_done")

        def pair(name):
            return [sem(f"{name}{b}") for b in range(B)]

        part0, rest0, part1, part2 = pair("part0"), pair("rest0"), pair("part1"), pair("part2")
        uparts_done = sem("uparts_done")
        x_part_done, xblk_ready, hist_saved = pair("x_part_done"), pair("xblk_ready"), pair("hist_saved")
        pre_done, gates_done, scores_done = pair("pre_done"), pair("gates_done"), pair("scores_done")
        tanh_done, exp_done, tzr_done, cand_done = pair("tanh_done"), pair("exp_done"), pair("tzr_done"), pair("cand_done")
        cols_done, nmax_done, rden_done, acc_zr = pair("cols_done"), pair("nmax_done"), pair("rden_done"), pair("acc_zr")
        base_done, half_h_done, omz_done, zh_done, h_done = (pair(n) for n in ("base_done", "half_h_done", "omz_done", "zh_done", "h_done"))

        pre = [bank[b][:, 0:S] for b in range(B)]
        gat = [bank[2 + b][:, 0:U * 12].rearrange("p (s g i) -> p s g i", g=4, i=3) for b in range(B)]
        sco = [bank[4 + b][:, 0:S] for b in range(B)]

        acc = [bank[4 + b][:, 160:162] for b in range(B)]
        hcand = [bank[2 + b][:, 128:129] for b in range(B)]

        block = ctx.enter_context(nc.Block())

        @block.sync
        def _(sp):
            sp.dma_start(x_tok[:], A["x"].rearrange("b (t p) d -> p (b t) d", p=128)).then_inc(ld_x, 16)
            sp.dma_start(ctx_tok[:], A["ctx_1024"].rearrange("b (c p) d -> p (b c) d", p=CP)).then_inc(ld_ctx, 16)
            sp.dma_start(w_att[:], A["L0_xcond_W_att"].rearrange("(two k) m -> k two m", two=2)).then_inc(ld_w, 16)
            sp.dma_start(v_col[:], A["L0_xcond_V_att"]).then_inc(ld_w, 16)
            sp.dma_start(wi[:], A["L0_xcond_Wi"].rearrange("(two k) m -> k two m", two=2)).then_inc(ld_w, 16)
            sp.dma_start(uh[:], A["L0_xcond_Uh"]).then_inc(ld_w, 16)
            with nc.allow_non_contiguous_dma(reason="few elements"):
                sp.dma_start(b_col[:], A["L0_xcond_b"].rearrange("(g d) -> d g", d=D)).then_inc(ld_w, 16)
                sp.dma_start(hring[:, :, U - 1], A["cond_1024"].rearrange("b d -> d b")).then_inc(ld_h0, 16)
            def row(name):
                return A[name].rearrange("(a n) -> a n", a=1)

            def col(name):
                return A[name].rearrange("(n a) -> n a", a=1)

            sp.dma_start(slot_tok, A["L0_ffn_slot_embeds"].rearrange("e s d -> (e s) d").rearrange("(t p) d -> p t d", p=128)).then_inc(Q["ld_slot"], 16)
            for k, n in enumerate("L0_ffn_slot_g L0_ffn_slot_b - L0_ffn_norm_g L0_ffn_norm_b L1_xcond_lnkv_g L1_xcond_lnkv_b "
                                  "L1_xcond_bk L1_xcond_bv L1_xcond_bq L1_xcond_b1 L1_xcond_lnq_g L1_xcond_lnq_b "
                                  "L1_xcond_lnm_g L1_xcond_lnm_b".split()):
                src = row("L0_ffn_scale").to_broadcast([128, 1]) if n == "-" else col(n)
                sp.dma_start(cols[:, k:k + 1], src).then_inc(Q["ld_cols"], 16)
            for t, n in ((wk, "wk"), (wv, "wv"), (wq, "wq"), (wus, "wu"), (w1, "w1"), (w2, "w2")):
                sp.dma_start(t[:], A["L1_xcond_" + n]).then_inc(Q["ld_c"], 16)
            sp.dma_start(bu_rep[:], row("L1_xcond_bu").to_broadcast([CP, D])).then_inc(Q["ld_rep"], 16)
            sp.dma_start(mu_rep[:], A["L1_xcond_q_mu"].rearrange("a b d -> (a b) d").to_broadcast([128, D])).then_inc(Q["ld_rep"], 16)
            sp.dma_start(sig_rep[:], A["L1_xcond_q_logsig"].rearrange("a b d -> (a b) d").to_broadcast([128, D])).then_inc(Q["ld_rep"], 16)
            for b in range(B):
                sp.dma_start(cls_rep[:, b, :], A["cond_1024"][b:b + 1, :].to_broadcast([128, D])).then_inc(Q["ld_rep"], 16)
            for t, n in ((b2_rep, "b2"), (pg_rep, "lnp_g"), (pb_rep, "lnp_b")):
                sp.dma_start(t[:], row("L1_xcond_" + n).to_broadcast([128, D])).then_inc(Q["ld_rep"], 16)
            sp.dma_start(sh_in, A["L1_ffn_w_in_shared_FD"].rearrange("(c p) d -> p c d", p=128)).then_inc(Q["ld_d"], 16)
            sp.dma_start(sh_sw, A["L1_ffn_w_swiglu_FD"].rearrange("(c p) d -> p c d", p=128)).then_inc(Q["ld_d"], 16)
            sp.dma_start(sh_out, A["L1_ffn_w_out_shared_DF"]).then_inc(Q["ld_d"], 16)
            sp.dma_start(router[:], A["L1_ffn_router_DE"]).then_inc(Q["ld_d"], 16)
            sp.dma_start(wg[:], A["L0_ffn_Wg"].rearrange("e d f -> d e f")).then_inc(Q["ld_exp"], 16)
            sp.dma_start(wu_[:], A["L0_ffn_Wu"].rearrange("e d f -> d e f")).then_inc(Q["ld_exp"], 16)
            sp.dma_start(wd[:], A["L0_ffn_Wd"].rearrange("e (c p) d -> p (e c) d", p=128)).then_inc(Q["ld_exp"], 16)
            with nc.allow_non_contiguous_dma(reason="few elements"):
                sp.dma_start(bg_col[:], A["L0_ffn_bg"].rearrange("e (c p) -> p (e c)", p=128)).then_inc(Q["ld_exp"], 16)
                sp.dma_start(bu_col[:], A["L0_ffn_bu"].rearrange("e (c p) -> p (e c)", p=128)).then_inc(Q["ld_exp"], 16)
            for half in range(2):
                sp.dma_start(bd_rep[64 * half:64 * half + 64, :, :],
                             A["L0_ffn_bd"].rearrange("(j two) d -> two j d", two=2)[half:half + 1].to_broadcast([64, NJ, D])).then_inc(Q["ld_exp"], 16)
            sp.wait_ge(Q["e_mm"], E0)
            sp.dma_start(win, A["L1_ffn_w_in_eDF"].rearrange("e d f -> d e f")).then_inc(Q["ld_moe"], 16)
            sp.dma_start(wsw, A["L1_ffn_w_swiglu_eDF"].rearrange("e d f -> d e f")).then_inc(Q["ld_moe"], 16)
            sp.dma_start(wout.rearrange("p e (c d) -> p (e c) d", c=FC), A["L1_ffn_w_out_eFD"].rearrange("e (c p) d -> p (e c) d", p=128)).then_inc(Q["ld_moe"], 16)
            sp.wait_ge(Q["res_done"], B)
            sp.dma_start(out.rearrange("b (t p) d -> p (b t) d", p=128), res).then_inc(out_done, 16)
            sp.wait_ge(out_done, 16)

        @block.gpsimd
        def _(pool):
            pool.memset(ident[:], 0.0).then_inc(consts_done, 1)
            pool.wait_ge(consts_done, 1)
            pool.affine_select(out=ident[:], in_=ident[:], compare_op=ALU.not_equal, fill=1.0, base=0,
                               pattern=[[-1, 128]], channel_multiplier=1).then_inc(consts_done, 1)
            pool.memset(vw[:, :, D:D + 1], 1.0).then_inc(consts_done, 1)
            pool.memset(zero_col[:], 0.0).then_inc(consts_done, 1)
            pool.memset(half_col[:], 0.5).then_inc(consts_done, 1)
            pool.memset(minus_half[:], -0.5).then_inc(consts_done, 1)
            pool.memset(xblk[:], 0.0).then_inc(consts_done, 1)
            pool.wait_ge(consts_done, N_CONSTS)
            norms = [0]

            def inverse_root(tiles, P=128):
                norms[0] += 1
                pool.wait_ge(var_ready, norms[0])
                sl = slice(tiles[0], tiles[-1] + 1)
                pool.tensor_tensor(rstd[0:P, sl], rs_v[0:P, sl], minus_half[0:P, sl], ALU.pow).then_inc(rstd_ready, 1)

            def inverse_roots():
                for b in range(B):
                    inverse_root(range(4 * b, 4 * b + 4))

            inverse_roots()
            inverse_roots()
            inverse_root(range(B * NCC), CP)
            pool.wait_ge(setup_ev, N_SETUP_EV)

            def next_inputs(b, t):
                pool.tensor_copy(xblk[:, b, :, 0:3, 0], xg[:, b, bass.ds(t, U), :]).then_inc(xblk_ready[b], U)

            def split_state(b, t, s):
                p = (s - 1) % U
                h = hring[:, b, p:p + 1]
                if isinstance(t, int) and t == 0:
                    pool.wait_ge(ld_h0, 16)
                else:
                    pool.wait_ge(h_done[b], t)
                    pool.wait_ge(gates_done[b], t)
                pool.tensor_tensor(h_part[:, b, 0:1], h, zero_col[:], ALU.add).then_inc(part0[b], 1)
                pool.wait_ge(part0[b], t + 1)
                pool.tensor_tensor(h_rest[:, b:b + 1], h, h_part[:, b, 0:1], ALU.subtract).then_inc(rest0[b], 1)
                pool.wait_ge(rest0[b], t + 1)
                pool.tensor_tensor(h_part[:, b, 1:2], h_rest[:, b:b + 1], zero_col[:], ALU.add).then_inc(part1[b], 1)
                pool.wait_ge(part1[b], t + 1)
                pool.tensor_tensor(h_part[:, b, 2:3], h_rest[:, b:b + 1], h_part[:, b, 1:2], ALU.subtract).then_inc(part2[b], 1)

            def halve(b, t, s):
                p = (s - 1) % U
                pool.tensor_tensor(half_h[:, b:b + 1], hring[:, b, p:p + 1], half_col[:], ALU.mult).then_inc(half_h_done[b], 1)

            def save(b, t):
                pool.tensor_copy(hist[:, b, bass.ds(t, U)], hring[:, b, :]).then_inc(hist_saved[b], U)

            def block_of_steps(t0, first=False, last=False):
                for s in range(U):
                    for b in range(B):
                        split_state(b, t0 + s, s)
                        halve(b, t0 + s, s)
                        if s == 0 and not first:
                            save(b, t0 - U)
                        if s == 1 and not last:
                            next_inputs(b, t0 + U)

            for b in range(B):
                next_inputs(b, 0)
            block_of_steps(0, first=True)
            with pool.Fori(1, T // U - 1) as k:
                block_of_steps(k * U)
            block_of_steps(T - U, last=True)
            for b in range(B):
                pool.wait_ge(h_done[b], T)
                pool.tensor_copy(hist[:, b, T - U:T], hring[:, b, :]).then_inc(hist_saved[b], U)
            inverse_roots()
            inverse_roots()
            inverse_roots()
            for it in range(ITERS):
                for b in range(B):
                    inverse_root(range(4 * b, 4 * b + 4))
                    pool.tensor_tensor(moved[:, 4 * b:4 * b + 4, :], slots[:, 4 * b:4 * b + 4, :],
                                       cls_rep[:, b, :].unsqueeze(1).to_broadcast([128, 4, D]), ALU.add).then_inc(moved_done[b], 1)
                inverse_roots()
                inverse_roots()

        @block.scalar
        def _(act):
            act.wait_ge(Q["ld_rep"], 16 * 8)
            act.activation(sig_rep[:], sig_rep[:], ACT.Exp).then_inc(Q["sig_done"], 1)

            def tanh_scores(b, t):
                act.wait_ge(pre_done[b], t + 1)
                act.activation(tanhT[:, b, :], pre[b], ACT.Tanh).then_inc(tanh_done[b], 1)

            def exp_scores(b, t):
                act.wait_ge(nmax_done[b], t + 1)
                act.activation(probs[:, b, 0:S], sco[b], ACT.Exp, bias=nmax[:, b:b + 1],
                               accum_out=probs[:, b, S:S + 1]).then_inc(exp_done[b], 1)

            def gate_zr(b, t):
                act.wait_ge(acc_zr[b], t + 1)
                act.activation(tzr[:, b, :], acc[b], ACT.Tanh, scale=rden[:, b:b + 1]).then_inc(tzr_done[b], 1)

            def candidate(b, t):
                act.wait_ge(base_done[b], t + 1)
                act.wait_ge(tzr_done[b], t + 1)
                act.activation(hcand[b], tzr[:, b, 1:2], ACT.Tanh, bias=base_h[:, b:b + 1],
                               scale=ewx[:, b, RH, S:S + 1]).then_inc(cand_done[b], 1)

            def block_of_steps(t0, first=False):
                for s in range(U):
                    t = t0 + s
                    tanh_scores(0, t)
                    if not (first and s == 0):
                        gate_zr(1, t - 1)
                        candidate(1, t - 1)
                    exp_scores(0, t)
                    tanh_scores(1, t)
                    gate_zr(0, t)
                    candidate(0, t)
                    exp_scores(1, t)

            block_of_steps(0, True)
            with act.Fori(1, T // U) as k:
                block_of_steps(k * U)
            gate_zr(1, T - 1)
            candidate(1, T - 1)

            def d_exp(k):
                act.wait_ge(Q["dmax_done"], k + 1)
                if k >= 3:
                    act.wait_ge(Q["dtr_done"], k - 2)
                act.activation(eD[:, k % 3, :], bank[k % 2], ACT.Exp, bias=dmax[:, k:k + 1],
                               accum_out=dsum[:, k:k + 1]).then_inc(Q["dexp_done"], 1)

            def d_copy(k):
                act.wait_ge(Q["dtr_done"], k + 1)
                if k >= 2:
                    act.wait_ge(Q["ds_done"], k - 1)
                act.activation(dT[:, k % 2, :], bank[2 + k % 2], ACT.Copy).then_inc(Q["dT_done"], 1)

            for k in range(B * NJ + 1):
                if k < B * NJ:
                    d_exp(k)
                if k >= 1:
                    d_copy(k - 1)

            def c_exp(m):
                act.wait_ge(Q["cmax_done"], m + 1)
                if m >= 2:
                    act.wait_ge(Q["ctr_done"], m - 1)
                p = (6, 0)[m % 2]
                act.activation(eC[:, m % 2, :], psum[:, p:p + 2, :].rearrange("p a n -> p (a n)"), ACT.Exp, bias=cmax[:, m:m + 1],
                               accum_out=csum[:, m:m + 1]).then_inc(Q["cexp_done"], 1)

            def c_copy(m):
                act.wait_ge(Q["ctr_done"], m + 1)
                b, i = m // 4, m % 4
                act.activation(eCT[:, b, 0:4, i * 128:(i + 1) * 128], bank[2 + 2 * (m % 2)].rearrange("p (j n) -> p j n", j=4),
                               ACT.Copy).then_inc(Q["cT_act"], 1)

            for m in range(NT + 1):
                if m < NT:
                    c_exp(m)
                if m >= 1:
                    c_copy(m - 1)

            act.wait_ge(Q["ld_exp"], 16 * 7)
            for e in range(E0):
                act.wait_ge(Q["e_mm"], e + 1)
                if e >= 2:
                    act.wait_ge(Q["egu"], e - 1)
                for f in range(FC):
                    ins = act.activation(ga[:, e % 2, f, :], bank[e % 2][:, f * 128:(f + 1) * 128], ACT.Gelu,
                                         bias=bg_col[:, e * FC + f:e * FC + f + 1])
                ins.then_inc(Q["egelu"], 1)

            for it in range(ITERS):
                for b in range(B):
                    act.wait_ge(CQ["q_tr"][b], it + 1)
                    act.activation(lnT[:, b, :], bank[4 * b], ACT.Identity, bias=qb_col, scale=qg_col).then_inc(CQ["q_lnT"][b], 1)
                for b in range(B):
                    act.wait_ge(CQ["q_mm"][b], it + 1)
                    act.activation(qT[:, b, :], bank[4 * b + 1], ACT.Identity, bias=bq_col).then_inc(CQ["q_T"][b], 1)
                for b in range(B):
                    act.wait_ge(CQ["amax"][b], it + 1)
                    for c in range(NCC):
                        ins = act.activation(attn[:, b, c, :], bank[4 * b + 2 + c][0:CP, :], ACT.Exp, bias=amax[:, b, c:c + 1],
                                             scale=QK_SCALE, accum_out=asum[:, b, c:c + 1])
                    ins.then_inc(CQ["exp"][b], 1)
                for b in range(B):
                    act.wait_ge(CQ["m_tr"][b], it + 1)
                    act.activation(lnT[:, b, :], bank[4 * b + 2], ACT.Identity, bias=mb_col, scale=mg_col).then_inc(CQ["m_lnT"][b], 1)
                    act.wait_ge(CQ["m_mm"][b], it + 1)
                    act.activation(gT[:, b, :], bank[4 * b + 3], ACT.Gelu, bias=b1_col).then_inc(CQ["gelu"][b], 1)

            for b in range(B):
                act.wait_ge(Q["tr_y"], b + 1)
                act.activation(yT[:, b, :], bank[b], ACT.Copy).then_inc(Q["yT_done"], 1)
            act.wait_ge(Q["r_mm"], 1)
            act.activation(gates[:].rearrange("p t e -> p (t e)"), bank[4][:, 0:NT * E1], ACT.Exp, scale=-1.0).then_inc(Q["gates_done_d"], 1)
            for u in range(2 * B * (E1 + 1)):
                act.wait_ge(Q["m_mm"], u + 1)
                if u >= 2:
                    act.wait_ge(Q["h_done_d"], u - 1)
                act.activation(sil[:, u % 2, :], bank[u % 2], ACT.Silu).then_inc(Q["silu_done"], 1)
            for b in range(B):
                act.wait_ge(Q["o_mm"], B * 2 * (E1 + 1) - 2 * (B - 1 - b))
                act.activation(outT[:, b, :], bank[6 + b], ACT.Copy).then_inc(Q["outT_done"], 1)

        @block.vector
        def _(dve):
            links = [0]

            def link(ins):
                links[0] += 1
                ins.then_inc(Q["dve_link"], 1)
                dve.wait_ge(Q["dve_link"], links[0])

            norms = [0]

            def moments(src, tiles, P=128, twice=False):
                for i in tiles:
                    ins = dve.bn_stats(stats[0:P, i, :], src[:, i, :])
                link(ins)
                for i in tiles:
                    ins = dve.bn_aggr(mv[0:P, i, :], stats[0:P, i, :])
                link(ins)
                scale, offset = (1.0 + EPS, EPS * EPS) if twice else (1.0, EPS)
                sl = slice(tiles[0], tiles[-1] + 1)
                dve.tensor_scalar(rs_v[0:P, sl], mv[0:P, sl, 1], scale, offset, ALU.mult, ALU.add).then_inc(var_ready, 1)
                norms[0] += 1
                return norms[0]

            def normalize(dst, src, tiles, norm, done, P=128):
                dve.wait_ge(rstd_ready, norm)
                for i in tiles:
                    ins = dve.tensor_scalar(dst[:, i, :], src[:, i, :], mv[0:P, i, 0:1], rstd[0:P, i:i + 1],
                                            ALU.subtract, ALU.mult)
                    if done is not None:
                        ins.then_inc(done, 1)
                if done is None:
                    link(ins)

            def layer_norm(dst, src, n, done, P=128, twice=False):
                parts = [range(n)] if n < NT else [range(0, n // 2), range(n // 2, n)]
                norm = [moments(src, p, P, twice) for p in parts]
                for p, k in zip(parts, norm):
                    normalize(dst, src, p, k, done, P)

            dve.wait_ge(ld_x, 16)
            layer_norm(xn_tok, x_tok, NT, xn_done)
            dve.wait_ge(ld_w, 16 * 5)
            dve.tensor_copy(v_rep[:], v_col[:].to_broadcast([D, D])).then_inc(halved, 1)
            dve.tensor_scalar(wi[:, :, 0:2 * D], wi[:, :, 0:2 * D], 0.5, None, ALU.mult).then_inc(halved, 1)
            dve.tensor_scalar(uh[:], uh[:], 0.5, None, ALU.mult).then_inc(halved, 1)
            dve.tensor_scalar(b_col[:, 0:2], b_col[:, 0:2], 0.5, None, ALU.mult).then_inc(halved, 1)
            dve.wait_ge(halved, 4)
            dve.tensor_copy(uh_part[:, 0, :], uh[:]).then_inc(uparts_done, 1)
            dve.wait_ge(uparts_done, 1)
            dve.tensor_tensor(uh_rest[:], uh[:], uh_part[:, 0, :], ALU.subtract).then_inc(uparts_done, 1)
            dve.wait_ge(uparts_done, 2)
            dve.tensor_copy(uh_part[:, 1, :], uh_rest[:]).then_inc(uparts_done, 1)
            dve.wait_ge(uparts_done, 3)
            dve.tensor_tensor(uh_part[:, 2, :], uh_rest[:], uh_part[:, 1, :], ALU.subtract).then_inc(uparts_done, 1)
            dve.wait_ge(setup_pe, 1)
            dve.tensor_copy(encT[:].rearrange("p b s -> p (b s)"), bank[6][:, 0:B * S]).then_inc(setup_ev, 1)
            for b in range(B):
                dve.wait_ge(setup_pe, 2 + b)
                dve.tensor_copy(xnT[:, b, :], bank[b][:, :]).then_inc(setup_ev, 1)
            for g in range(3):
                dve.wait_ge(setup_pe, 4 + g)
                dve.tensor_copy(ewx[:, :, g, 0:S], bank[2 + g][:, 0:B * S].rearrange("p (b s) -> p b s", b=B)).then_inc(setup_ev, 1)

            for b in range(B):
                for g in range(3):
                    dve.wait_ge(setup_pe, 7 + b * 3 + g)
                    dve.tensor_scalar(xg[:, b, :, g], bank[(6, 7, 0, 1, 5, 6)[b * 3 + g]][:], b_col[:, g:g + 1], None, ALU.add).then_inc(setup_ev, 1)

            dve.wait_ge(Q["ld_slot"], 16)
            layer_norm(slot_nrm, slot_tok, NJ, Q["pre_ev"])
            dve.wait_ge(ld_ctx, 16)
            layer_norm(ctxn, ctx_tok, B * NCC, Q["pre_ev"], P=CP)
            dve.wait_ge(Q["ld_cols"], 16 * 15)
            link(dve.tensor_scalar(cols[:, 0:2], cols[:, 0:2], scale_col, None, ALU.mult))
            for h in range(2):
                dve.wait_ge(Q["pre_tr"], 1 + h)
                dve.tensor_scalar(seT[:, h * 512:(h + 1) * 512], bank[h], sg_col, sbias_col, ALU.mult, ALU.add).then_inc(Q["pre_ev"], 1)
            dve.wait_ge(Q["pre_tr"], 3)
            dve.tensor_scalar(ctxnT[:], bank[2][:, 0:B * S], kvg_col, kvb_col, ALU.mult, ALU.add).then_inc(Q["pre_ev"], 1)
            dve.wait_ge(Q["ld_rep"], 16 * 8)
            dve.tensor_tensor(cls_rep[:], cls_rep[:], b2_rep[:].unsqueeze(1).to_broadcast([128, B, D]), ALU.add).then_inc(Q["pre_ev"], 1)
            dve.wait_ge(consts_done, 2)
            dve.tensor_copy(ident16[:], ident[:])
            link(dve.tensor_tensor(sel_col[:], ident[0:3 * E1, 0:E1], ident[0:3 * E1, E1:2 * E1], ALU.add))
            link(dve.tensor_tensor(sel_col[:], sel_col[:], ident[0:3 * E1, 2 * E1:3 * E1], ALU.add))
            dve.tensor_copy(sel[:], sel_col[:].unsqueeze(2).to_broadcast([3 * E1, E1, 128])).then_inc(Q["pre_ev"], 1)
            dve.wait_ge(Q["pre_tr"], 4)
            dve.tensor_scalar(kT[:], bank[3][:, 0:B * S], bk_col, None, ALU.add).then_inc(Q["pre_ev"], 1)
            dve.wait_ge(Q["pre_tr"], 5)
            dve.tensor_scalar(vT[:], bank[4][:, 0:B * S], bv_col, None, ALU.add).then_inc(Q["pre_ev"], 1)
            dve.wait_ge(Q["pre_tr"], 6)
            dve.tensor_tensor(vw[:, :, 0:D], bank[5][0:CP, :].rearrange("p (i d) -> p i d", i=B * NCC),
                              bu_rep[:].unsqueeze(1).to_broadcast([CP, B * NCC, D]), ALU.add).then_inc(Q["pre_ev"], 1)
            dve.wait_ge(Q["pre_tr"], 7)
            dve.tensor_copy(sh_turned[:, 0:2, :], bank[6].rearrange("p (c f) -> p c f", c=2)).then_inc(Q["pre_ev"], 1)
            dve.tensor_copy(sh_turned[:, 2, :], bank[7][:, 0:F]).then_inc(Q["pre_ev"], 1)
            def columns(b, t, s):
                dve.wait_ge(gates_done[b], t + 1)
                dve.tensor_reduce(ewx[:, b, :, S:S + 1].rearrange("p g o -> p (g o)"), gat[b][:, s, :, :], AX.X, ALU.add).then_inc(cols_done[b], 1)

            def row_max(b, t):
                dve.wait_ge(scores_done[b], t + 1)
                dve.tensor_reduce(nmax[:, b:b + 1], sco[b], AX.X, ALU.max, negate=True).then_inc(nmax_done[b], 1)

            def attend(b, t):
                dve.wait_ge(exp_done[b], t + 1)
                dve.reciprocal(rden[:, b:b + 1], probs[:, b, S:S + 1]).then_inc(rden_done[b], 1)
                dve.wait_ge(cols_done[b], t + 1)
                for g in (GZ, GR):
                    ins = dve.tensor_tensor_reduce(junk[:, b, g, :], probs[:, b, :], ewx[:, b, g, :], 1.0, 0.0, ALU.mult, ALU.add,
                                                   acc[b][:, g:g + 1])
                ins.then_inc(acc_zr[b], 1)
                dve.wait_ge(rden_done[b], t + 1)
                dve.tensor_tensor_reduce(junk[:, b, GH, :], probs[:, b, :], ewx[:, b, GH, :], rden[:, b:b + 1], 0.0, ALU.mult, ALU.add,
                                         base_h[:, b:b + 1]).then_inc(base_done[b], 1)

            def keep(b, t, s):
                dve.wait_ge(tzr_done[b], t + 1)
                dve.tensor_scalar(omz[:, b:b + 1], tzr[:, b, 0:1], -0.5, 0.5, ALU.mult, ALU.add).then_inc(omz_done[b], 1)
                dve.wait_ge(half_h_done[b], t + 1)
                dve.scalar_tensor_tensor(out=zh[:, b:b + 1], in0=tzr[:, b, 0:1], scalar=half_h[:, b:b + 1],
                                         in1=half_h[:, b:b + 1], op0=ALU.mult, op1=ALU.add).then_inc(zh_done[b], 1)

            def new_state(b, t, s):
                dve.wait_ge(cand_done[b], t + 1)
                dve.wait_ge(omz_done[b], t + 1)
                dve.wait_ge(zh_done[b], t + 1)
                if s == 0:
                    if not (isinstance(t, int) and t == 0):
                        dve.wait_ge(hist_saved[b], t)
                dve.scalar_tensor_tensor(out=hring[:, b, s:s + 1], in0=hcand[b], scalar=omz[:, b:b + 1],
                                         in1=zh[:, b:b + 1], op0=ALU.mult, op1=ALU.add).then_inc(h_done[b], 1)

            def block_of_steps(t0, first=False):
                for s in range(U):
                    t = t0 + s
                    q = (s - 1) % U
                    if not (first and s == 0):
                        attend(1, t - 1)
                        keep(1, t - 1, q)
                    row_max(0, t)
                    if not (first and s == 0):
                        new_state(1, t - 1, q)
                    columns(0, t, s)
                    attend(0, t)
                    keep(0, t, s)
                    row_max(1, t)
                    new_state(0, t, s)
                    columns(1, t, s)

            dve.wait_ge(ld_h0, 16)
            block_of_steps(0, True)
            with dve.Fori(1, T // U) as k:
                block_of_steps(k * U)
            attend(1, T - 1)
            keep(1, T - 1, U - 1)
            new_state(1, T - 1, U - 1)

            for b in range(B):
                dve.wait_ge(Q["tr_b"], b + 1)
                ins = dve.tensor_tensor(x1[:, 4 * b:4 * b + 4, :], x_tok[:, 4 * b:4 * b + 4, :],
                                        bank[6 + b].rearrange("p (t d) -> p t d", t=4), ALU.add)
            link(ins)
            layer_norm(xB, x1, NT, Q["xB_done"], twice=True)
            for b in range(B):
                dve.wait_ge(Q["tr_b"], 3 + b)
                dve.tensor_scalar(xBT[:, b, :], bank[b], ng_col, nb_col, ALU.mult, ALU.add).then_inc(Q["xBT_done"], 1)

            def d_max(k):
                dve.wait_ge(Q["lt_done"], k + 1)
                dve.tensor_reduce(dmax[:, k:k + 1], bank[k % 2], AX.X, ALU.max, negate=True).then_inc(Q["dmax_done"], 1)

            def d_norm(k):
                dve.wait_ge(Q["dexp_done"], k + 1)
                link(dve.reciprocal(drec[:, k:k + 1], dsum[:, k:k + 1]))
                dve.tensor_scalar(eD[:, k % 3, :], eD[:, k % 3, :], drec[:, k:k + 1], None, ALU.mult).then_inc(Q["dnorm_done"], 1)

            def d_slots(k):
                b, j = k // NJ, k % NJ
                dve.wait_ge(Q["ds_done"], k + 1)
                dve.tensor_scalar(slotsT[:, 2 * j:2 * j + 2, b, :], bank[4 + k % 2][:, 0:128].rearrange("p (e s) -> p e s", e=2),
                                  ng_col, nb_col, ALU.mult, ALU.add).then_inc(Q["slots_ev"], 1)

            for k in range(B * NJ + 3):
                if k < B * NJ:
                    d_max(k)
                if 1 <= k <= B * NJ:
                    d_norm(k - 1)
                if k >= 3:
                    d_slots(k - 3)

            def c_max(m):
                p = (6, 0)[m % 2]
                dve.wait_ge(Q["l_done"], m + 1)
                dve.tensor_reduce(cmax[:, m:m + 1], psum[:, p:p + 2, :], AX.XY, ALU.max, negate=True).then_inc(Q["cmax_done"], 1)

            def c_copy(m):
                b, i = m // 4, m % 4
                dve.wait_ge(Q["ctr_done"], m + 1)
                dve.tensor_copy(eCT[:, b, 4:8, i * 128:(i + 1) * 128],
                                bank[3 + 2 * (m % 2)].rearrange("p (j n) -> p j n", j=4)).then_inc(Q["cT_dve"], 1)

            for m in range(NT + 1):
                if m < NT:
                    c_max(m)
                if m >= 1:
                    c_copy(m - 1)
            dve.wait_ge(Q["cexp_done"], NT)
            link(dve.reciprocal(crec[:], csum[:]))

            def expert_bias(j):
                dve.wait_ge(Q["eo_mm"], 2 * j + 2)
                dve.tensor_tensor(eo[:, j, :, :], bank[4 + j % 2][:, 0:B * D].rearrange("p (b d) -> p b d", b=B),
                                  bd_rep[:, j, :].unsqueeze(1).to_broadcast([128, B, D]), ALU.add).then_inc(Q["eo_ev"], 1)

            dve.wait_ge(Q["ld_exp"], 16 * 7)
            for e in range(E0):
                dve.wait_ge(Q["egelu"], e + 1)
                if e >= 2:
                    dve.wait_ge(Q["eo_mm"], e - 1)
                for f in range(FC):
                    ins = dve.scalar_tensor_tensor(out=gu[:, e % 2, f, :], in0=bank[2 + e % 2][:, f * 128:(f + 1) * 128],
                                                   scalar=bu_col[:, e * FC + f:e * FC + f + 1], in1=ga[:, e % 2, f, :],
                                                   op0=ALU.add, op1=ALU.mult)
                ins.then_inc(Q["egu"], 1)
                if e >= 2 and e % 2 == 0:
                    expert_bias(e // 2 - 1)
            expert_bias(NJ - 1)
            for m in range(NT):
                dve.wait_ge(Q["cm_mm"], m + 1)
                dve.scalar_tensor_tensor(out=x2[:, m, :], in0=bank[6 + m % 2][:, 0:D], scalar=crec[:, m:m + 1], in1=x1[:, m, :],
                                         op0=ALU.mult, op1=ALU.add).then_inc(Q["x2_done"], 1)
            dve.wait_ge(Q["x2_done"], NT)

            tiles = [range(4 * b, 4 * b + 4) for b in range(B)]
            layer_norm(lnt, x2, NT, None)
            dve.wait_ge(Q["sig_done"], 1)
            link(dve.tensor_tensor(slots, lnt, sig_rep[:].unsqueeze(1).to_broadcast([128, NT, D]), ALU.mult))
            link(dve.tensor_tensor(slots, slots, mu_rep[:].unsqueeze(1).to_broadcast([128, NT, D]), ALU.add))
            norm = [moments(slots, tiles[b]) for b in range(B)]
            for it in range(ITERS):
                for b in range(B):
                    normalize(lnt, slots, tiles[b], norm[b], CQ["q_ln"][b])
                for b in range(B):
                    dve.wait_ge(CQ["log_mm"][b], it + 1)
                    link(dve.tensor_reduce(amax[:, b, :], psum[0:CP, 4 * b + 2:4 * b + 4, :], AX.X, ALU.max, negate=True))
                    dve.tensor_scalar(amax[:, b, :], amax[:, b, :], QK_SCALE, None, ALU.mult).then_inc(CQ["amax"][b], 1)
                for b in range(B):
                    dve.wait_ge(CQ["exp"][b], it + 1)
                    link(dve.reciprocal(arec[:, b, :], asum[:, b, :]))
                    for c in range(NCC):
                        ins = dve.tensor_scalar(attn[:, b, c, :], attn[:, b, c, :], arec[:, b, c:c + 1], EPS_ATTN, ALU.mult, ALU.add)
                    ins.then_inc(CQ["attn"][b], 1)
                for b in range(B):
                    dve.wait_ge(CQ["upd_mm"][b], it + 1)
                    upd = psum[:, 4 * b:4 * b + 2, 0:2 * (D + 1)].rearrange("p a (k d) -> p a k d", k=2)
                    link(dve.reciprocal(urec[:, b, :].rearrange("p (a k) -> p a k", k=2), upd[:, :, :, D]))
                    for k in range(4):
                        ins = dve.scalar_tensor_tensor(out=slots[:, 4 * b + k, :], in0=upd[:, k // 2, k % 2, 0:D],
                                                       scalar=urec[:, b, k:k + 1], in1=slots[:, 4 * b + k, :],
                                                       op0=ALU.mult, op1=ALU.add)
                    link(ins)
                    normalize(lnt, slots, tiles[b], moments(slots, tiles[b]), CQ["m_ln"][b])
                for b in range(B):
                    sl = slots[:, 4 * b:4 * b + 4, :]
                    dve.wait_ge(moved_done[b], it + 1)
                    dve.wait_ge(CQ["w2_mm"][b], it + 1)
                    link(dve.tensor_tensor(sl, moved[:, 4 * b:4 * b + 4, :], bank[4 * b].rearrange("p (k d) -> p k d", k=4), ALU.add))
                    norm[b] = moments(slots, tiles[b])
                    for i in tiles[b]:
                        ins = dve.scalar_tensor_tensor(out=lnt[:, i, :], in0=slots[:, i, :], scalar=mv[:, i, 0:1], in1=pg_rep[:],
                                                       op0=ALU.subtract, op1=ALU.mult)
                    ins.then_inc(centred[b], 1)
                for b in range(B):
                    dve.wait_ge(centred[b], it + 1)
                    dve.wait_ge(rstd_ready, norm[b])
                    for i in tiles[b]:
                        ins = dve.scalar_tensor_tensor(out=slots[:, i, :], in0=lnt[:, i, :], scalar=rstd[:, i:i + 1], in1=pb_rep[:],
                                                       op0=ALU.mult, op1=ALU.add)
                    link(ins)
                    if it + 1 < ITERS:
                        norm[b] = moments(slots, tiles[b])

            for b in range(B):
                link(dve.tensor_tensor(x3[:, 4 * b:4 * b + 4, :], x2[:, 4 * b:4 * b + 4, :], slots[:, 4 * b:4 * b + 4, :], ALU.add))
                norm[b] = moments(x3, tiles[b])
            for b in range(B):
                normalize(lnt, x3, tiles[b], norm[b], Q["yn_done"])
            dve.wait_ge(Q["r_mm"], 1)
            dve.wait_ge(Q["gates_done_d"], 1)
            link(dve.tensor_copy(sc[:].rearrange("p t e -> p (t e)"), bank[4][:, 0:NT * E1]))
            link(dve.tensor_scalar(gates[:], gates[:], 1.0, None, ALU.add))
            link(dve.reciprocal(gates[:], gates[:]))

            def route(q):
                dve.wait_ge(Q["rep_mm"], q + 1 - B)
                if q >= B + 2:
                    dve.wait_ge(Q["m_mm"], 2 * (q - 1))
                dve.tensor_tensor(routed[:, q % 2, :], yT[:, q % B, :], bank[4 + q % 2], ALU.mult).then_inc(Q["routed_done"], 1)

            def gated(u):
                dve.wait_ge(Q["silu_done"], u + 1)
                if u >= 2:
                    dve.wait_ge(Q["o_mm"], u - 1)
                dve.tensor_tensor(hT[:, u % 2, :], sil[:, u % 2, :], bank[2 + u % 2], ALU.mult).then_inc(Q["h_done_d"], 1)

            link(dve.memset(rank[:], 0.0))
            for j in range(E1):
                if j + 1 < E1:
                    ins = dve.tensor_tensor(beats[:, :, j + 1:], sc[:, :, j:j + 1].to_broadcast([128, NT, E1 - 1 - j]), sc[:, :, j + 1:], ALU.is_ge)
                if j:
                    ins = dve.tensor_tensor(beats[:, :, 0:j], sc[:, :, j:j + 1].to_broadcast([128, NT, j]), sc[:, :, 0:j], ALU.is_gt)
                link(ins)
                if j + 1 < E1:
                    ins = dve.tensor_tensor(rank[:, :, j + 1:], rank[:, :, j + 1:], beats[:, :, j + 1:], ALU.add)
                if j:
                    ins = dve.tensor_tensor(rank[:, :, 0:j], rank[:, :, 0:j], beats[:, :, 0:j], ALU.add)
                link(ins)
                if j % 2:
                    gated(j // 2)
            link(dve.scalar_tensor_tensor(out=gates[:], in0=rank[:], scalar=float(TOP_K), in1=gates[:], op0=ALU.is_lt, op1=ALU.mult))
            link(dve.tensor_copy(gate_part[:, :, 0, :], gates[:]))
            link(dve.tensor_tensor(gate_rest[:], gates[:], gate_part[:, :, 0, :], ALU.subtract))
            link(dve.tensor_copy(gate_part[:, :, 1, :], gate_rest[:]))
            dve.tensor_tensor(gate_part[:, :, 2, :], gate_rest[:], gate_part[:, :, 1, :], ALU.subtract).then_inc(Q["gates_done_d"], 1)
            for b in range(B):
                dve.wait_ge(Q["tr_g"], b + 1)
                dve.tensor_copy(gTr[:, b, :], bank[4 + b][0:3 * E1, :]).then_inc(Q["gTr_done"], 1)
            route(B)
            for q in range(B, B * (E1 + 1)):
                if q + 1 < B * (E1 + 1):
                    route(q + 1)
                gated(2 * q)
                gated(2 * q + 1)
            for b in range(B):
                dve.wait_ge(Q["tr_o"], b + 1)
                dve.tensor_tensor(res[:, 4 * b:4 * b + 4, :], x3[:, 4 * b:4 * b + 4, :], bank[b].rearrange("p (t d) -> p t d", t=4),
                                  ALU.add).then_inc(Q["res_done"], 1)

        @block.tensor
        def _(pe):
            pe.wait_ge(consts_done, N_CONSTS)
            pe.wait_ge(ld_ctx, 16)
            for i in range(B * NCC):
                ins = pe.transpose(bank[6][:, i * CP:(i + 1) * CP], ctx_tok[:, i, :], ident[0:CP, 0:CP])
            ins.then_inc(setup_pe, 1)
            for i in range(NT):
                pe.wait_ge(xn_done, i + 1)
                ins = pe.transpose(bank[i // 4][:, (i % 4) * 128:(i % 4 + 1) * 128], xn_tok[:, i, :], ident[:])
                if i % 4 == 3:
                    ins.then_inc(setup_pe, 1)
            pe.wait_ge(halved, 4)
            pe.wait_ge(setup_ev, 1)
            pe.wait_ge(setup_ev, 3)
            for g in range(3):
                pe.matmul(bank[2 + g][:, 0:B * S], wi[:, 1, g * D:(g + 1) * D], encT[:].rearrange("p b s -> p (b s)"),
                          start=True, stop=True).then_inc(setup_pe, 1)

            for b in range(B):
                for g in range(3):
                    i = b * 3 + g
                    pe.wait_ge(setup_ev, (1, 1, 3, 3, 6, 7)[i])
                    pe.matmul(bank[(6, 7, 0, 1, 5, 6)[i]][:], wi[:, 0, g * D:(g + 1) * D], xnT[:, b, :],
                              start=True, stop=True).then_inc(setup_pe, 1)

            pe.wait_ge(setup_ev, N_SETUP_EV)
            for i in range(NJ):
                pe.wait_ge(Q["pre_ev"], i + 1)
                ins = pe.transpose(bank[i // 4][:, (i % 4) * 128:(i % 4 + 1) * 128], slot_nrm[:, i, :], ident[:])
                if i % 4 == 3:
                    ins.then_inc(Q["pre_tr"], 1)
            for i in range(B * NCC):
                pe.wait_ge(Q["pre_ev"], NJ + i + 1)
                ins = pe.transpose(bank[2][:, i * CP:(i + 1) * CP], ctxn[:, i, :], ident[0:CP, 0:CP])
            ins.then_inc(Q["pre_tr"], 1)
            pe.wait_ge(Q["ld_c"], 16 * 6)
            pe.wait_ge(Q["pre_ev"], PRE_CTXT)
            pe.matmul(bank[3][:, 0:B * S], wk[:], ctxnT[:], start=True, stop=True).then_inc(Q["pre_tr"], 1)
            pe.matmul(bank[4][:, 0:B * S], wv[:], ctxnT[:], start=True, stop=True).then_inc(Q["pre_tr"], 1)
            pe.wait_ge(Q["pre_ev"], PRE_V)
            for i in range(B * NCC):
                ins = pe.matmul(bank[5][0:CP, i * D:(i + 1) * D], vT[:, i * CP:(i + 1) * CP], wus[:], start=True, stop=True)
            ins.then_inc(Q["pre_tr"], 1)
            pe.wait_ge(Q["ld_d"], 16 * 4)
            for c in range(FC):
                pe.transpose(bank[6][:, c * 128:(c + 1) * 128], sh_in[:, c, :], ident[:])
                pe.transpose(bank[6][:, F + c * 128:F + (c + 1) * 128], sh_sw[:, c, :], ident[:])
                ins = pe.transpose(bank[7][:, c * 128:(c + 1) * 128], sh_out[:, c * 128:(c + 1) * 128], ident[:])
            ins.then_inc(Q["pre_tr"], 1)
            pe.wait_ge(Q["pre_ev"], PRE_ALL)

            def refresh(b, t):
                if not (isinstance(t, int) and t == 0):
                    pe.wait_ge(tanh_done[b], t)
                pe.matmul(pre[b], w_att[:, 1, :], encT[:, b, :], start=True, stop=False, skip_group_check=True)

            def x_part(b, t):
                pe.wait_ge(xblk_ready[b], t + U)
                pe.matmul(gat[b].rearrange("p s g i -> p (s g i)"), ident[:], xblk[:, b].rearrange("p s g i -> p (s g i)"), start=True, stop=False,
                          skip_group_check=True).then_inc(x_part_done[b], U)

            def keep_clock(n):
                for _ in range(n):
                    pe.matmul(bank[6], uh_part[:, 0, 0:D], uh_part[:].rearrange("p i m -> p (i m)")[:, 0:512], start=True, stop=True)

            def query(b, t, s):
                p = (s - 1) % U
                if isinstance(t, int) and t == 0:
                    pe.wait_ge(ld_h0, 16)
                else:
                    pe.wait_ge(h_done[b], t)
                pe.matmul(pre[b], w_att[:, 0, :], hring[:, b, p:p + 1].to_broadcast([D, S]), start=False, stop=True,
                          skip_group_check=True).then_inc(pre_done[b], 1)

            def h_gates(b, t, s):
                pe.wait_ge(part2[b], t + 1)
                for c, g in ((GZ, 0), (GR, 1), (GH, 2), (RH, 2)):
                    for i in range(3):
                        ins = pe.matmul(gat[b][:, s, c, i:3], uh_part[:, i, g * D:(g + 1) * D], h_part[:, b, 0:3 - i],
                                        start=False, stop=True, skip_group_check=True)
                ins.then_inc(gates_done[b], 1)

            def scores(b, t):
                pe.wait_ge(tanh_done[b], t + 1)
                pe.matmul(sco[b], v_rep[:], tanhT[:, b, :], start=True, stop=True).then_inc(scores_done[b], 1)

            def block_of_steps(t0, first=False, last=False):
                for s in range(U):
                    t = t0 + s
                    query(0, t, s)
                    refresh(1, t)
                    scores(0, t)
                    if s == 0:
                        x_part(0, t)
                    h_gates(0, t, s)
                    keep_clock(1)
                    query(1, t, s)
                    if not (last and s == U - 1):
                        refresh(0, t + 1)
                    scores(1, t)
                    if s == 0:
                        x_part(1, t)
                    h_gates(1, t, s)
                    keep_clock(1)

            pe.wait_ge(setup_ev, N_SETUP_EV)
            pe.wait_ge(uparts_done, 4)
            pe.wait_ge(consts_done, N_CONSTS)
            keep_clock(10)
            refresh(0, 0)
            block_of_steps(0, first=True)
            with pe.Fori(1, T // U - 1) as k:
                block_of_steps(k * U)
            block_of_steps(T - U, last=True)

            def turn(dst, tiles, done=None, step=None):
                for i, tile in enumerate(tiles):
                    if done is not None:
                        pe.wait_ge(done, step + i + 1)
                    ins = pe.transpose(dst[:, i * 128:(i + 1) * 128], tile, ident[:])
                return ins

            for b in range(B):
                pe.wait_ge(hist_saved[b], T)
                turn(bank[6 + b], [hist[:, b, i * 128:(i + 1) * 128] for i in range(4)]).then_inc(Q["tr_b"], 1)
            for b in range(B):
                turn(bank[b], [xB[:, 4 * b + i, :] for i in range(4)], Q["xB_done"], 4 * b).then_inc(Q["tr_b"], 1)

            def d_logits(k):
                b, j = k // NJ, k % NJ
                pe.wait_ge(Q["xBT_done"], b + 1 if k >= 2 else 2)
                if k >= 2:
                    pe.wait_ge(Q["dexp_done"], k - 1)
                pe.matmul(bank[k % 2], seT[:, j * 128:(j + 1) * 128], xBT[:, b, :], start=True, stop=True).then_inc(Q["lt_done"], 1)

            def d_turn(k):
                pe.wait_ge(Q["dnorm_done"], k + 1)
                if k >= 2:
                    pe.wait_ge(Q["dT_done"], k - 1)
                turn(bank[2 + k % 2], [eD[:, k % 3, i * 128:(i + 1) * 128] for i in range(4)]).then_inc(Q["dtr_done"], 1)

            def d_slots(k):
                b = k // NJ
                pe.wait_ge(Q["dT_done"], k + 1)
                if k >= 2:
                    pe.wait_ge(Q["slots_ev"], k - 1)
                for i in range(4):
                    ins = pe.matmul(bank[4 + k % 2][:, 0:128], xB[:, 4 * b + i, :], dT[:, k % 2, i * 128:(i + 1) * 128],
                                    start=(i == 0), stop=(i == 3))
                ins.then_inc(Q["ds_done"], 1)

            d_logits(0)
            for k in range(B * NJ + 2):
                if k + 1 < B * NJ:
                    d_logits(k + 1)
                if 1 <= k <= B * NJ:
                    d_turn(k - 1)
                if k >= 2:
                    d_slots(k - 2)

            def c_logits(m):
                b, i = m // 4, m % 4
                p = (6, 0)[m % 2]
                if m == 1:
                    pe.wait_ge(Q["dexp_done"], B * NJ)
                if m >= 2:
                    pe.wait_ge(Q["cexp_done"], m - 1)
                for h in range(2):
                    ins = pe.matmul(bank[p + h], xBT[:, b, i * 128:(i + 1) * 128], seT[:, h * 512:(h + 1) * 512], start=True, stop=True)
                ins.then_inc(Q["l_done"], 1)

            def c_turn(m):
                pe.wait_ge(Q["cexp_done"], m + 1)
                if m == 0:
                    pe.wait_ge(Q["dT_done"], B * NJ)
                if m == 1:
                    pe.wait_ge(Q["slots_ev"], B * NJ)
                if m >= 2:
                    pe.wait_ge(Q["cT_act"], m - 1)
                    pe.wait_ge(Q["cT_dve"], m - 1)
                for h in range(2):
                    ins = turn(bank[2 + 2 * (m % 2) + h], [eC[:, m % 2, (4 * h + i) * 128:(4 * h + i + 1) * 128] for i in range(4)])
                ins.then_inc(Q["ctr_done"], 1)

            for m in range(NT + 1):
                if m < NT:
                    c_logits(m)
                if m >= 1:
                    c_turn(m - 1)

            def e_in(e):
                if e == 0:
                    pe.wait_ge(Q["ld_exp"], 16 * 7)
                    pe.wait_ge(Q["slots_ev"], B * NJ)
                    pe.wait_ge(Q["cexp_done"], NT)
                    pe.wait_ge(Q["cT_act"], NT)
                    pe.wait_ge(Q["cT_dve"], NT)
                if e >= 2:
                    pe.wait_ge(Q["egelu"], e - 1)
                    pe.wait_ge(Q["egu"], e - 1)
                x = slotsT[:, e].rearrange("p b s -> p (b s)")
                for f in range(FC):
                    pe.matmul(bank[e % 2][:, f * 128:(f + 1) * 128], wg[:, e, f * 128:(f + 1) * 128], x, start=True, stop=True)
                    ins = pe.matmul(bank[2 + e % 2][:, f * 128:(f + 1) * 128], wu_[:, e, f * 128:(f + 1) * 128], x, start=True, stop=True)
                ins.then_inc(Q["e_mm"], 1)

            def e_out(e):
                j, r = e // 2, 64 * (e % 2)
                pe.wait_ge(Q["egu"], e + 1)
                if j >= 2:
                    pe.wait_ge(Q["eo_ev"], j - 1)
                for b in range(B):
                    for f in range(FC):
                        ins = pe.matmul(bank[4 + j % 2][r:r + 64, b * D:(b + 1) * D], gu[:, e % 2, f, b * SL0:(b + 1) * SL0],
                                        wd[:, e * FC + f, :], start=(f == 0), stop=(f == FC - 1), skip_group_check=True)
                ins.then_inc(Q["eo_mm"], 1)

            for e in range(E0 + 1):
                if e < E0:
                    e_in(e)
                if e >= 1:
                    e_out(e - 1)
            pe.wait_ge(Q["eo_ev"], NJ)
            for m in range(NT):
                b, i = m // 4, m % 4
                if m >= 2:
                    pe.wait_ge(Q["x2_done"], m - 1)
                for j in range(NJ):
                    ins = pe.matmul(bank[6 + m % 2][:, 0:D], eCT[:, b, j, i * 128:(i + 1) * 128], eo[:, j, b, :],
                                    start=(j == 0), stop=(j == NJ - 1))
                ins.then_inc(Q["cm_mm"], 1)

            for it in range(ITERS):
                for b in range(B):
                    turn(bank[4 * b], [lnt[:, 4 * b + i, :] for i in range(4)], CQ["q_ln"][b], 4 * it).then_inc(CQ["q_tr"][b], 1)
                for b in range(B):
                    pe.wait_ge(CQ["q_lnT"][b], it + 1)
                    pe.matmul(bank[4 * b + 1], wq[:], lnT[:, b, :], start=True, stop=True).then_inc(CQ["q_mm"][b], 1)
                for b in range(B):
                    pe.wait_ge(CQ["q_T"][b], it + 1)
                    for c in range(NCC):
                        ins = pe.matmul(bank[4 * b + 2 + c][0:CP, :], kT[:, (b * NCC + c) * CP:(b * NCC + c + 1) * CP], qT[:, b, :],
                                        start=True, stop=True)
                    ins.then_inc(CQ["log_mm"][b], 1)
                for b in range(B):
                    pe.wait_ge(CQ["attn"][b], it + 1)
                    for k in range(4):
                        for c in range(NCC):
                            ins = pe.matmul(bank[4 * b + k // 2][:, (k % 2) * (D + 1):(k % 2 + 1) * (D + 1)],
                                            attn[:, b, c, k * 128:(k + 1) * 128], vw[:, b * NCC + c, :],
                                            start=(c == 0), stop=(c == NCC - 1))
                    ins.then_inc(CQ["upd_mm"][b], 1)
                for b in range(B):
                    turn(bank[4 * b + 2], [lnt[:, 4 * b + i, :] for i in range(4)], CQ["m_ln"][b], 4 * it).then_inc(CQ["m_tr"][b], 1)
                    pe.wait_ge(CQ["m_lnT"][b], it + 1)
                    pe.matmul(bank[4 * b + 3], w1[:], lnT[:, b, :], start=True, stop=True).then_inc(CQ["m_mm"][b], 1)
                    pe.wait_ge(CQ["gelu"][b], it + 1)
                    for k in range(4):
                        ins = pe.matmul(bank[4 * b][:, k * 128:(k + 1) * 128], gT[:, b, k * 128:(k + 1) * 128], w2[:],
                                        start=True, stop=True)
                    ins.then_inc(CQ["w2_mm"][b], 1)

            for b in range(B):
                turn(bank[b], [lnt[:, 4 * b + i, :] for i in range(4)], Q["yn_done"], 4 * b).then_inc(Q["tr_y"], 1)
            pe.wait_ge(Q["yT_done"], 2)
            for i in range(NT):
                ins = pe.matmul(bank[4][:, i * E1:(i + 1) * E1], yT[:, i // 4, (i % 4) * 128:(i % 4 + 1) * 128], router[:],
                                start=True, stop=True)
            ins.then_inc(Q["r_mm"], 1)

            def turn_gates():
                pe.wait_ge(Q["gates_done_d"], 2)
                for i in range(NT):
                    ins = pe.matmul(bank[4 + i // 4][0:3 * E1, (i % 4) * 128:(i % 4 + 1) * 128],
                                    gate_part[:, i].rearrange("p k e -> p (k e)"), ident16[:], start=True, stop=True)
                    if i % 4 == 3:
                        ins.then_inc(Q["tr_g"], 1)
                pe.wait_ge(Q["gTr_done"], 2)

            order = [E1] + list(range(E1))

            def replicate(q):
                if q >= B + 2:
                    pe.wait_ge(Q["routed_done"], q - 1 - B)
                pe.matmul(bank[4 + q % 2], sel[:, order[q // B], :], gTr[:, q % B, :], start=True, stop=True).then_inc(Q["rep_mm"], 1)

            def d_in(u):
                q, f = u // 2, u % 2
                e = order[q // B]
                x = yT[:, q % B, :] if q < B else routed[:, q % 2, :]
                w_in, w_sw = (sh_turned[:, 0, :], sh_turned[:, 1, :]) if q < B else (win[:, e, :], wsw[:, e, :])
                if q >= B:
                    pe.wait_ge(Q["routed_done"], q + 1 - B)
                if q == B:
                    pe.wait_ge(Q["ld_moe"], 16 * 3)
                if u >= 2:
                    pe.wait_ge(Q["silu_done"], u - 1)
                    pe.wait_ge(Q["h_done_d"], u - 1)
                pe.matmul(bank[u % 2], w_in[:, f * 128:(f + 1) * 128], x, start=True, stop=True)
                pe.matmul(bank[2 + u % 2], w_sw[:, f * 128:(f + 1) * 128], x, start=True, stop=True).then_inc(Q["m_mm"], 1)

            def d_out(u):
                q, f = u // 2, u % 2
                e = order[q // B]
                pe.wait_ge(Q["h_done_d"], u + 1)
                w_o = sh_turned[:, 2, :] if q < B else wout[:, e, :]
                pe.matmul(bank[6 + q % B], w_o[:, f * 128:(f + 1) * 128], hT[:, u % 2, :], start=(q < B and f == 0),
                          stop=(q // B == E1 and f == 1), skip_group_check=True).then_inc(Q["o_mm"], 1)

            NU = 2 * B * (E1 + 1)
            for u in range(NU + 2):
                if u < NU:
                    if u == 2 * B:
                        turn_gates()
                        replicate(B)
                    if u % 2 == 0 and B < u // 2 + 1 < B * (E1 + 1):
                        replicate(u // 2 + 1)
                    d_in(u)
                if u >= 2:
                    d_out(u - 2)
            for b in range(B):
                pe.wait_ge(Q["outT_done"], b + 1)
                turn(bank[b], [outT[:, b, i * 128:(i + 1) * 128] for i in range(4)]).then_inc(Q["tr_o"], 1)


def kernel(**inputs):
    import numpy as np
    import concourse.bacc as bacc
    from concourse import mybir as mb
    from concourse.bass_utils import run_bass_kernel_spmd as run
    nc = bacc.Bacc("TRN2", target_bir_lowering=False, num_devices=1)
    arrays, aps = {}, {}
    for name, a in inputs.items():
        a = np.ascontiguousarray(a)
        arrays[f"in_{name}"] = a
        aps[name] = nc.dram_tensor(f"in_{name}", a.shape, mb.dt.from_np(a.dtype), kind="ExternalInput").ap()
    out = nc.dram_tensor("out_0", (2, 512, 128), mb.dt.float32, kind="ExternalOutput").ap()
    build(nc, aps, out)
    r = run(nc, [arrays], core_ids=[0])
    return r.results[0]["out_0"]
```
